# Optimizing a Trainium2 kernel written in Bass

```python
import numpy as np
import jax
import jax.numpy as jnp

def _softmax(x, axis=-1):
    return jax.nn.softmax(x, axis=axis)

def _gelu(x):
    return jax.nn.gelu(x, approximate=True)

def _silu(x):
    return jax.nn.silu(x)

def _sigmoid(x):
    return jax.nn.sigmoid(x)

def _layernorm(x, axis=-1, eps=1e-05):
    m = jnp.mean(x, axis=axis, keepdims=True)
    v = jnp.var(x, axis=axis, keepdims=True)
    return (x - m) / jnp.sqrt(v + eps)

def _scatter_add(tgt, idx, src, axis=0):
    return tgt.at[idx].add(src)

def _segment_sum(src, seg, n):
    return jax.ops.segment_sum(src, seg, n)
kernel_name = 'mk_gnn_preln_d1_gnn_r64_d209f4'

def setup_inputs(seed: int=0):
    np.random.seed(seed)
    _w = jnp.asarray

    def _rec_inputs():
        import jax
        import jax.numpy as jnp
        _gk = jax.random.key(seed)
        x = -0.0001126 + 1 * jax.random.normal(jax.random.fold_in(_gk, 1), (50000, 256), jnp.float32)
        src = jax.random.randint(jax.random.fold_in(_gk, 2), (12500,), 0, 50000, jnp.int32)
        dst = jax.random.randint(jax.random.fold_in(_gk, 3), (12500,), 0, 50000, jnp.int32)
        _o = jnp.argsort(dst, stable=True)
        src = src[_o]
        dst = dst[_o]
        edge_type_8 = jax.random.randint(jax.random.fold_in(_gk, 12), (12500,), 0, 8, jnp.int32)
        return (x, src, dst, edge_type_8)
    x, src, dst, edge_type_8 = _rec_inputs()

    def _L0_gnn_setup():
        import jax, jax.numpy as jnp
        import numpy as np
        N = 30000
        E = 9375
        FIN = 256
        FOUT = 256
        R = 8
        key = jax.random.key(seed)
        ks = jax.random.split(key, 6)
        x = jax.random.normal(ks[0], (N, FIN), dtype=jnp.float32)
        W = jax.random.normal(ks[1], (R, FIN, FOUT), dtype=jnp.float32) * (1.0 / np.sqrt(FIN))
        W_root = jax.random.normal(ks[2], (FIN, FOUT), dtype=jnp.float32) * (1.0 / np.sqrt(FIN))
        bias = jax.random.normal(ks[3], (FOUT,), dtype=jnp.float32) * 0.01
        edge_index = jax.random.randint(ks[4], (2, E), 0, N, dtype=jnp.int64)
        edge_type = jax.random.randint(ks[5], (E,), 0, R, dtype=jnp.int64)
        return {'x': x, 'W': W, 'W_root': W_root, 'bias': bias, 'edge_index': edge_index, 'edge_type': edge_type}
    _L0_gnn_all = _L0_gnn_setup()
    _L0_gnn_in = {k: v for k, v in _L0_gnn_all.items() if k in ('W', 'W_root', 'bias')}
    del _L0_gnn_all
    return {'x': x, 'src': src, 'dst': dst, 'edge_type_8': edge_type_8, 'L0_gnn_W': _L0_gnn_in['W'], 'L0_gnn_W_root': _L0_gnn_in['W_root'], 'L0_gnn_bias': _L0_gnn_in['bias']}

def reference(x, src, dst, edge_type_8, L0_gnn_W, L0_gnn_W_root, L0_gnn_bias):
    import jax
    import jax.numpy as jnp

    def _L0_gnn_ref(x, W, W_root, bias, edge_index, edge_type):
        import jax, jax.numpy as jnp
        import numpy as np
        N = 30000
        E = 9375
        FIN = 256
        FOUT = 256
        R = 8
        n, fin = x.shape
        r = W.shape[0]
        src, dst = (edge_index[0], edge_index[1])
        seg = dst * r + edge_type
        sums = jax.ops.segment_sum(x[src], seg, num_segments=n * r)
        cnt = jax.ops.segment_sum(jnp.ones_like(src, dtype=x.dtype), seg, num_segments=n * r)
        mean = (sums / jnp.maximum(cnt, 1.0)[:, None]).reshape(n, r, fin)
        out = jnp.einsum('nri,rio->no', mean, W) + x @ W_root + bias
        return jax.nn.relu(out)
    edge_index = jnp.stack([src, dst])
    h = jnp.maximum(_layernorm(x, axis=-1), 0.0)
    x = x + _L0_gnn_ref(h, L0_gnn_W, L0_gnn_W_root, L0_gnn_bias, edge_index, edge_type_8)
    return x

_drawn_inputs = setup_inputs


def setup_inputs(seed=0):
    import zlib

    import numpy as np

    out = dict(_drawn_inputs(seed))
    spreads = {}
    factors = {'L0_gnn_bias': 8.0}
    for name, (base, spread) in spreads.items():
        noise = np.random.default_rng([zlib.crc32(name.encode()), seed]).standard_normal(out[name].shape)
        drawn = base * np.exp(spread * noise) if base else spread * noise
        out[name] = jnp.asarray(drawn.astype(out[name].dtype))
    for name, factor in factors.items():
        out[name] = (out[name] * factor).astype(out[name].dtype)
    return out
```

```python
from contextlib import ExitStack

import concourse.bass as bass
from concourse import mybir

F32 = mybir.dt.float32
BF16 = mybir.dt.bfloat16
I32 = mybir.dt.int32
ALU = mybir.AluOpType
ACT = mybir.ActivationFunctionType
AX_X = mybir.AxisListType.X

P = 128
UNROLL = 3
DENSE, PAIRS = 4, 2
EDGE = 3
BIG = 1 << 20
EPS = 1e-05
MSG, AGG, ROOT = range(3)


def cdiv(a, b):
    return -(-a // b)


class Plan:

    def __init__(self, n, f, e, r):
        self.N, self.F, self.E, self.R = n, f, e, r
        self.GROUP = P * DENSE
        self.STEPS = cdiv(n, self.GROUP)
        self.BLOCK = P - 1
        self.BLOCKS = cdiv(e, self.BLOCK)
        self.TILES = (e + r * (P - 1)) // P
        self.MSG_STEPS = cdiv(self.TILES, EDGE)
        self.AGG_STEPS = cdiv(self.BLOCKS, EDGE)
        assert self.TILES == EDGE * self.MSG_STEPS and self.BLOCKS == EDGE * self.AGG_STEPS
        self.AGG0 = self.MSG_STEPS
        self.ROOT0 = self.AGG0 + self.AGG_STEPS
        assert self.ROOT0 < self.STEPS

    def kind(self, s):
        return MSG if s < self.AGG0 else AGG if s < self.ROOT0 else ROOT


class Step:

    def __init__(self, plan, base, turn=None):
        self.plan, self.base, self.turn = plan, base, turn
        self.slot = base % UNROLL
        self.kind = plan.kind(base)
        self.next_kind = plan.kind(base + 1)

    def lin(self, a, c):
        return a * self.base + c if self.turn is None else self.turn * (a * UNROLL) + (a * self.base + c)

    def use(self, scale, c, first=0):
        n = (self.base - first) // UNROLL
        return scale * n + c if self.turn is None else self.turn * scale + (scale * n + c)

    def jobs(self):
        if self.kind == ROOT:
            return [(0, 0, None, 0), (1, 1, None, 1)]
        return [(0, 0, None, 0), (1, None, 0, 1), (2, 1, None, 0), (3, None, 1, 1), (4, None, 2, 2)]

    def job(self, pos, c=0):
        if self.kind == ROOT:
            root0 = self.plan.ROOT0
            return self.lin(PAIRS, (EDGE + PAIRS) * root0 - PAIRS * root0 + pos + c)
        return self.lin(EDGE + PAIRS, pos + c)

    def tiles(self, kind):
        return DENSE if kind == ROOT else DENSE + EDGE

    def after(self, k):
        return Step(self.plan, self.base + k, self.turn)


def run_steps(eng, plan, body, ends=None):
    def peeled(a, b):
        for s in range(a, b):
            body(Step(plan, s))

    def looped(a, b):
        turns = (b - a) // UNROLL
        if turns < 2:
            return peeled(a, b)
        with eng.Fori(0, turns) as turn:
            for c in range(UNROLL):
                body(Step(plan, a + c, turn))
        peeled(a + UNROLL * turns, b)

    a, b, c = plan.AGG0, plan.ROOT0, plan.STEPS
    first = a % UNROLL or UNROLL
    peeled(0, first)
    looped(first, a - UNROLL)
    peeled(a - UNROLL, a + UNROLL)
    looped(a + UNROLL, b - UNROLL)
    peeled(b - UNROLL, b)
    if ends == b:
        return
    peeled(b, b + UNROLL)
    looped(b + UNROLL, c - 2 * UNROLL)
    peeled(c - 2 * UNROLL, c)


def build(nc, x, src, dst, etype, W, W_root, bias, out):
    N, F = x.shape
    R = W.shape[0]
    E = src.shape[0]
    KC = F // P
    pl = Plan(N, F, E, R)
    BLOCK, BLOCKS, TILES, STEPS = pl.BLOCK, pl.BLOCKS, pl.TILES, pl.STEPS
    AGG0, ROOT0 = pl.AGG0, pl.ROOT0
    COLS = TILES + BLOCKS
    LASTROW = N - pl.GROUP
    PAD = N + 10000
    assert F == 2 * P and PAD + 1 < (1 << 16) and TILES <= P and BLOCKS <= P

    ctx = ExitStack()
    with ctx:
        def sb(name, shape, dt=F32):
            return ctx.enter_context(nc.sbuf_tensor(name, shape, dt))

        early = ExitStack()

        def pre(name, shape, dt=F32):
            return early.enter_context(nc.sbuf_tensor(name, shape, dt))

        def ps(name, shape, dt=F32):
            return ctx.enter_context(nc.psum_tensor(name, shape, dt))

        def sem(name):
            return ctx.enter_context(nc.semaphore(name))

        msgs = nc.dram_tensor("msgs", [TILES * P, F], F32, kind="Internal").ap()

        w_sb = sb("w_sb", [P, KC * R * F])
        wr_sb = sb("wr_sb", [P, KC, F])
        ident = sb("ident", [P, P])
        eps = sb("eps", [P, 1])
        bias_rows = sb("bias_rows", [P, 2, F], BF16)
        ones3 = sb("ones3", [P, P], BF16)
        ones3_agg = sb("ones3_agg", [P, P], BF16)
        cold = sb("cold", [P, BLOCKS])
        cole = sb("cole", [P, BLOCKS])
        gidx = sb("gidx", [P, COLS], I32)
        midx = sb("midx", [P, BLOCKS], I32)
        oidx = sb("oidx", [P, BLOCKS], I32)
        wcol = sb("wcol", [P, TILES])
        tile_type_i = sb("tile_type_i", [1, TILES], I32)
        need_i = sb("need_i", [1, 2, BLOCKS], I32)
        xin = [sb(f"xin{u}", [P, DENSE, F]) for u in range(UNROLL)]
        xout = [sb(f"xout{u}", [P, DENSE, F]) for u in range(UNROLL)]
        xg = [sb(f"xg{u}", [P, EDGE, F]) for u in range(UNROLL)]
        mbuf = [sb(f"mbuf{u}", [P, EDGE, F]) for u in range(UNROLL)]
        smat = [sb(f"smat{u}", [P, EDGE, P]) for u in range(UNROLL)]
        gslot = [sb(f"gslot{u}", [P, EDGE], I32) for u in range(UNROLL)]
        mslot = [sb(f"mslot{u}", [P, EDGE], I32) for u in range(UNROLL)]
        eslot = [sb(f"eslot{u}", [P, EDGE]) for u in range(UNROLL)]
        raw = sb("raw", [P, DENSE + EDGE, 6])
        mv = sb("mv", [P, DENSE + EDGE, 2])
        std = sb("std", [P, DENSE + EDGE])
        rstd = [sb(f"rstd{u}", [P, DENSE + EDGE]) for u in range(UNROLL)]
        nmean = [sb(f"nmean{u}", [P, DENSE + EDGE]) for u in range(UNROLL)]
        h = [sb(f"h{v}", [P, 2, F]) for v in range(3)]
        hT = [sb(f"hT{v}", [P, 2 * KC, P]) for v in range(3)]
        upper = pre("upper", [P, P])
        ones = pre("ones", [P, P])
        iota_i = pre("iota_i", [P, P], I32)
        iota_f = pre("iota_f", [P, P])
        bias3 = pre("bias3", [3, F])
        bpart = pre("bpart", [3, 3, F], BF16)
        bres = pre("bres", [3, F])
        rowd_i = pre("rowd_i", [BLOCKS, P + 1], I32)
        rows_i = pre("rows_i", [BLOCKS, P], I32)
        rowt_i = pre("rowt_i", [BLOCKS, P], I32)
        rowd = pre("rowd", [BLOCKS, P + 1])
        rows = pre("rows", [BLOCKS, P])
        rowt = pre("rowt", [BLOCKS, P])
        rowe = pre("rowe", [BLOCKS, P])
        rowx = pre("rowx", [BLOCKS, P])
        rowo = pre("rowo", [BLOCKS, P])
        rowg = pre("rowg", [BLOCKS, P])
        rowk = pre("rowk", [BLOCKS, P])
        onehot = pre("onehot", [BLOCKS, R, BLOCK])
        notfirst = pre("notfirst", [BLOCKS, R, BLOCK])
        rank = pre("rank", [BLOCKS, R, BLOCK])
        types_i = pre("types_i", [P, R], I32)
        types = pre("types", [P, R])
        total = pre("total", [P, 8, R])
        total_i = pre("total_i", [P, 2, R], I32)
        rowp = pre("rowp", [BLOCKS, P])
        rowp_i = pre("rowp_i", [BLOCKS, 3, P], I32)
        rowpf = pre("rowpf", [BLOCKS, 2, P])
        cols_ = pre("cols_", [P, BLOCKS])
        colk = pre("colk", [P, BLOCKS])
        coll = pre("coll", [P, BLOCKS])
        colq = pre("colq", [P, BLOCKS])
        lanes = pre("lanes", [P, 2, P])
        tiles2 = pre("tiles2", [P, 2, 2, TILES])
        keyc = pre("keyc", [P, TILES])
        keyr = pre("keyr", [TILES, P])
        same = pre("same", [TILES, P + 1])
        runf = pre("runf", [TILES, P])
        runt = pre("runt", [TILES, P])
        gate = pre("gate", [TILES, P])
        ends = pre("ends", [1, 4, TILES])
        link_row = pre("link_row", [1, 6, TILES + 1])
        carryc = pre("carryc", [TILES, 2])
        tile_type = pre("tile_type", [1, 2, TILES])
        need = pre("need", [1, 2, BLOCKS])
        early.close()
        orow = sb("orow", [P, BLOCKS, F])

        psT = [ps(f"psT{v}", [P, 2 * KC, P]) for v in range(3)]
        psO = [ps(f"psO{v}", [P, 2, F]) for v in range(3)]
        psR = ps("psR", [P, 512])
        psP = ps("psP", [P, 512])
        turned_rows = (psP, psR)

        s_w = sem("s_w")
        s_bias = sem("s_bias")
        s_list = sem("s_list")
        s_fill = sem("s_fill")
        s_pool = sem("s_pool")
        s_c = sem("s_c")
        s_pp = sem("s_pp")
        s_pv = sem("s_pv")
        s_lane = sem("s_lane")
        s_perm = sem("s_perm")
        s_prep = sem("s_prep")
        s_eps = sem("s_eps")
        x_in = [sem(f"x_in{u}") for u in range(UNROLL)]
        x_out = [sem(f"x_out{u}") for u in range(UNROLL)]
        g_in = [sem(f"g_in{u}") for u in range(UNROLL)]
        m_in = [sem(f"m_in{u}") for u in range(UNROLL)]
        m_out = [sem(f"m_out{u}") for u in range(UNROLL)]
        idx_ready = sem("idx_ready")
        fetches = sem("fetches")
        e_slot = sem("e_slot")
        bn_raw = sem("bn_raw")
        stats = sem("stats")
        std_ready = sem("std_ready")
        inv_ready = sem("inv_ready")
        nm_ready = sem("nm_ready")
        ln_ready = sem("ln_ready")
        normed = sem("normed")
        turned = sem("turned")
        hT_ready = sem("hT_ready")
        prods = sem("prods")
        fin = sem("fin")
        spread = sem("spread")
        s_ready = sem("s_ready")
        carry = sem("carry")
        rows_out = sem("rows_out")
        s_scat = sem("s_scat")

        block = ctx.enter_context(nc.Block())

        def node_rows(t, st):
            if st.turn is None:
                r0 = min(st.base * pl.GROUP, LASTROW)
                v = t[r0:r0 + pl.GROUP, :]
            else:
                v = t[bass.ds(st.lin(pl.GROUP, 0), pl.GROUP), :]
            return v.rearrange("(p j) f -> p (j f)", p=P)

        def flat(t):
            return t[:, :, :].rearrange("p a b -> p (a b)")

        @block.sync
        def _(sp):
            LAST = BLOCKS - 1
            TAIL = E - (BLOCK * LAST - 1)
            sp.wait_ge(s_fill, 3)
            n_list = 0
            for row, lst, width in ((rowd_i, dst, P + 1), (rows_i, src, P), (rowt_i, etype, P)):
                body = bass.AP(tensor=lst.tensor, offset=BLOCK - 1, ap=[[BLOCK, LAST - 1], [1, width]])
                sp.dma_start(row[1:LAST, 0:width], body).then_inc(s_list, 16)
                sp.dma_start(row[0:1, 1:width],
                             lst[0:width - 1].rearrange("(a c) -> a c", a=1)).then_inc(s_list, 16)
                sp.dma_start(row[LAST:LAST + 1, 0:TAIL],
                             lst[E - TAIL:E].rearrange("(a c) -> a c", a=1)).then_inc(s_list, 16)
            b1 = bias.rearrange("(a c) -> a c", a=1)
            for j in range(3):
                sp.dma_start(bias3[j:j + 1, :], b1).then_inc(s_bias, 16)
            for u in range(UNROLL):
                sp.dma_start(flat(xin[u]), node_rows(x, Step(pl, u))).then_inc(x_in[u], 16)
            for k in range(KC):
                sp.dma_start(wr_sb[:, k, :], W_root[k * P:(k + 1) * P, :]).then_inc(s_w, 16)
                sp.dma_start(w_sb[:, k * R * F:(k + 1) * R * F].rearrange("p (r o) -> p r o", r=R),
                             W[:, k * P:(k + 1) * P, :].rearrange("r p o -> p r o")).then_inc(s_w, 16)

            def relay(st):
                sp.wait_ge(x_out[st.slot], st.use(16, 16))
                sp.sem_inc(rows_out, 1)

            def body(st):
                u = st.slot
                pos = 1 if st.kind == ROOT else 2
                sp.wait_ge(fin, st.job(pos, 1))
                last = st.turn is None and st.base == STEPS - 1
                if last:
                    relay(st.after(-1))
                sp.dma_start(node_rows(out, st), flat(xout[u])).then_inc(x_out[u], 16)
                if st.turn is not None or st.base + UNROLL < STEPS:
                    sp.dma_start(flat(xin[u]), node_rows(x, st.after(UNROLL))).then_inc(x_in[u], 16)
                if st.kind == MSG:
                    sp.wait_ge(fin, st.job(4, 1))
                    sp.dma_start(msgs[bass.ds(st.lin(EDGE * P, 0), EDGE * P), :].rearrange("(k p) f -> p k f", k=EDGE),
                                 mbuf[u][:, :, :]).then_inc(m_out[u], 16)
                if not last and not (st.turn is None and st.base == 0):
                    relay(st.after(-1))

            run_steps(sp, pl, body)
            relay(Step(pl, STEPS - 1))

        @block.gpsimd
        def _(pool):
            nc.gpsimd.memset(rowd_i[:, :], PAD).then_inc(s_fill, 1)
            nc.gpsimd.memset(rows_i[:, :], 0).then_inc(s_fill, 1)
            nc.gpsimd.memset(rowt_i[:, :], R).then_inc(s_fill, 1)
            nc.gpsimd.iota(iota_i[:, :], [[1, P]], base=0, channel_multiplier=0).then_inc(s_pool, 1)
            nc.gpsimd.iota(types_i[:, :], [[1, R]], base=0, channel_multiplier=0).then_inc(s_pool, 1)
            nc.gpsimd.memset(ident[:, :], 0.0).then_inc(s_pool, 1)
            nc.gpsimd.memset(upper[:, :], 0.0).then_inc(s_pool, 1)
            nc.gpsimd.memset(ones[:, :], 1.0).then_inc(s_pool, 1)
            nc.gpsimd.memset(notfirst[:, :, :], 1.0).then_inc(s_pool, 1)
            nc.gpsimd.memset(eps[:, :], EPS).then_inc(s_eps, 1)
            pool.wait_ge(s_pool, 6)
            nc.gpsimd.affine_select(out=ident[:, :], in_=ident[:, :], compare_op=ALU.not_equal, fill=1.0,
                                    base=0, pattern=[[-1, P]], channel_multiplier=1).then_inc(s_pool, 1)
            nc.gpsimd.affine_select(out=upper[:, :], in_=upper[:, :], compare_op=ALU.is_ge, fill=1.0,
                                    base=0, pattern=[[-1, P]], channel_multiplier=1).then_inc(s_pool, 1)
            nc.gpsimd.memset(notfirst[:, :, 0:1], 0.0).then_inc(s_pool, 1)
            copies = [0]

            def slot_indices(slot, cols):
                nc.gpsimd.tensor_copy(slot[:, :], cols).then_inc(idx_ready, 1)

            def gather_x(st):
                u = st.slot
                for k in range(EDGE):
                    nc.gpsimd.indirect_dma_start(
                        out=xg[u][:, k, :], out_offset=None, in_=x[:, :],
                        in_offset=bass.IndirectOffsetOnAxis(ap=gslot[u][:, k:k + 1], axis=0)).then_inc(g_in[u], 16)

            def gather_m(st):
                u = st.slot
                for k in range(EDGE):
                    nc.gpsimd.indirect_dma_start(
                        out=mbuf[u][:, k, :], out_offset=None, in_=msgs[:, :],
                        in_offset=bass.IndirectOffsetOnAxis(ap=mslot[u][:, k:k + 1], axis=0)).then_inc(m_in[u], 16)

            def x_copies(st):
                if st.kind == MSG or (st.turn is None and st.base < AGG0 + UNROLL):
                    return st.lin(1, 1)
                return st.lin(2, 2 - 1 - AGG0)

            def m_copies(st):
                if st.turn is None and st.base < AGG0 + UNROLL:
                    return AGG0 + UNROLL + (st.base - AGG0) + 1
                return st.lin(2, 2 - AGG0)

            def fetch_x(st):
                slot_indices(gslot[st.slot], gidx[:, bass.ds(st.lin(EDGE, 0), EDGE)])
                pool.wait_ge(idx_ready, x_copies(st))
                pool.sem_inc(fetches, 1)
                gather_x(st)

            def fetch_m(st):
                slot_indices(mslot[st.slot], midx[:, bass.ds(st.lin(EDGE, -EDGE * AGG0), EDGE)])
                nc.gpsimd.tensor_copy(eslot[st.slot][:, :],
                                      cole[:, bass.ds(st.lin(EDGE, -EDGE * AGG0), EDGE)]).then_inc(e_slot, 1)
                pool.wait_ge(idx_ready, m_copies(st))
                pool.sem_inc(fetches, 1)
                gather_m(st)

            pool.wait_ge(s_prep, 1)
            for u in range(UNROLL):
                fetch_x(Step(pl, u))

            def body(st):
                if st.kind == ROOT:
                    return
                nxt = st.after(UNROLL)
                if st.turn is None and nxt.base >= ROOT0:
                    return
                pool.wait_ge(fin, st.job(4, 1))
                fetch_x(nxt)
                if st.kind == AGG:
                    fetch_m(nxt)
                elif st.turn is None and st.base == AGG0 - 1:
                    for u in range(UNROLL):
                        pool.wait_ge(m_out[u], Step(pl, AGG0 - UNROLL + (u - AGG0) % UNROLL).use(16, 16))
                    for v in range(UNROLL):
                        fetch_m(Step(pl, AGG0 + v))

            run_steps(pool, pl, body, ends=ROOT0)
            for b in range(BLOCKS):
                if b == 0:
                    pool.wait_ge(fin, Step(pl, ROOT0 - 1).job(4, 1))
                steps_needed = nc.gpsimd.value_load(need_i[0:1, 1, b:b + 1], min_val=1, max_val=STEPS)
                pool.wait_ge(rows_out, steps_needed)
                pool.sem_inc(fetches, 1)
                nc.gpsimd.indirect_dma_start(
                    out=out[:, :], out_offset=bass.IndirectOffsetOnAxis(ap=oidx[:, b:b + 1], axis=0),
                    in_=orow[:, b, :], in_offset=None, bounds_check=N - 1, oob_is_err=False).then_inc(s_scat, 16)
            pool.wait_ge(s_scat, 16 * BLOCKS)

        @block.scalar
        def _(act):
            act.wait_ge(s_eps, 1)

            def deviations(st):
                n = st.tiles(st.kind)
                act.wait_ge(stats, st.lin(1, 1))
                nc.scalar.activation(std[:, 0:n], mv[:, 0:n, 1], ACT.Sqrt, bias=eps[:, 0:1]).then_inc(std_ready, 1)

            def norm(st, j):
                pos, pair, edge, v = j
                u = st.slot
                if pos == 0:
                    act.wait_ge(ln_ready, st.lin(1, 1))
                if not (st.turn is None and st.base == 0 and pos < 2):
                    act.wait_ge(turned, st.job(pos, -1))
                if pair is None:
                    t = DENSE + edge
                    ins = nc.scalar.activation(h[v][:, 0, :], xg[u][:, edge, :], ACT.Relu,
                                               scale=rstd[u][:, t:t + 1], bias=nmean[u][:, t:t + 1])
                else:
                    for c in range(2):
                        t = 2 * pair + c
                        ins = nc.scalar.activation(h[v][:, c, :], xin[u][:, t, :], ACT.Relu,
                                                   scale=rstd[u][:, t:t + 1], bias=nmean[u][:, t:t + 1])
                ins.then_inc(normed, 1)

            def evacuate(st, j):
                pos, pair, edge, v = j
                act.wait_ge(turned, st.job(pos, 1))
                if not (st.turn is None and st.base == 0 and pos < 2):
                    act.wait_ge(prods, st.job(pos, -1))
                n = KC if pair is None else 2 * KC
                nc.scalar.activation(hT[v][:, 0:n, :], psT[v][:, 0:n, :], ACT.Copy).then_inc(hT_ready, 1)

            def body(st):
                jobs = st.jobs()
                nxt = st.after(1)
                last = st.turn is None and st.base == STEPS - 1
                for i, j in enumerate(jobs):
                    evacuate(st, j)
                    if i == len(jobs) // 2 and not last:
                        deviations(nxt)
                    if i + 1 < len(jobs):
                        norm(st, jobs[i + 1])
                    elif not last:
                        norm(nxt, nxt.jobs()[0])

            deviations(Step(pl, 0))
            norm(Step(pl, 0), Step(pl, 0).jobs()[0])
            run_steps(act, pl, body)

        @block.vector
        def _(dve):
            chain = [0]

            def link(ins):
                chain[0] += 1
                ins.then_inc(s_c, 1)
                dve.wait_ge(s_c, chain[0])

            V = nc.vector
            pe_done = [0]

            def from_pe():
                pe_done[0] += 1
                dve.wait_ge(s_pp, pe_done[0])

            def to_pe(ins):
                ins.then_inc(s_pv, 1)

            dve.wait_ge(s_pool, 9)
            link(V.tensor_copy(iota_f[:, :], iota_i[:, :]))
            link(V.tensor_copy(types[:, :], types_i[:, :]))
            dve.wait_ge(s_bias, 48)
            link(V.memset(bias_rows[:, :, :], 0.0))
            link(V.tensor_copy(bpart[:, 0, :], bias3[:, :]))
            link(V.tensor_tensor(bres[:, :], bias3[:, :], bpart[:, 0, :], ALU.subtract))
            link(V.tensor_copy(bpart[:, 1, :], bres[:, :]))
            link(V.tensor_tensor(bres[:, :], bres[:, :], bpart[:, 1, :], ALU.subtract))
            link(V.tensor_copy(bpart[:, 2, :], bres[:, :]))
            link(V.tensor_scalar(bres[:, :], bpart[:, 0, :], ident[0:3, 0:1], None, ALU.mult))
            for k in (1, 2):
                link(V.scalar_tensor_tensor(out=bres[:, :], in0=bpart[:, k, :], scalar=ident[0:3, k:k + 1],
                                            in1=bres[:, :], op0=ALU.mult, op1=ALU.add))
            for t in range(2):
                link(V.tensor_copy(bias_rows[0:3, t, :], bres[:, :]))
            link(V.memset(ones3[:, :], 0.0))
            link(V.memset(ones3[0:3, :], 1.0))
            link(V.tensor_copy(ones3_agg[:, :], ones3[:, :]))
            link(V.memset(ones3_agg[:, 0:1], 0.0))

            dve.wait_ge(s_list, 16 * 9)
            link(V.tensor_copy(rowd[:, :], rowd_i[:, :]))
            link(V.tensor_copy(rows[:, :], rows_i[:, :]))
            link(V.tensor_copy(rowt[:, :], rowt_i[:, :]))
            link(V.tensor_copy(rowe[:, :], rowd[:, 0:P]))
            link(V.tensor_copy(rowe[:, 0:1], rowd[:, P - 1:P]))
            link(V.tensor_tensor(rowx[:, :], rowd[:, 0:P], rowd[:, 1:P + 1], ALU.is_equal))
            link(V.scalar_tensor_tensor(out=rowo[:, :], in0=rowx[:, :], scalar=float(BIG), in1=rowd[:, 0:P],
                                        op0=ALU.mult, op1=ALU.add))
            link(V.memset(rowo[:, 0:1], float(BIG)))
            link(V.tensor_scalar(rowg[:, :], rowd[:, 0:P], float(N - 1), None, ALU.min))
            link(V.scalar_tensor_tensor(out=rowk[:, :], in0=rowt[:, :], scalar=65536.0, in1=rowd[:, 0:P],
                                        op0=ALU.mult, op1=ALU.add))
            link(V.tensor_scalar(rowk[:, :], rowk[:, :], 1.0, None, ALU.add))

            tb = rowt[:, 1:P].rearrange("b (a j) -> b a j", a=1).broadcast_to([BLOCKS, R, BLOCK])
            yb = types[0:BLOCKS, :].rearrange("b (r a) -> b r a", a=1).broadcast_to([BLOCKS, R, BLOCK])
            link(V.tensor_tensor(onehot[:, :, :], tb, yb, ALU.is_equal))
            link(V.tensor_tensor_scan(flat(rank), flat(notfirst), flat(onehot), 0.0, ALU.mult, ALU.add))
            rowtot = total[0:BLOCKS, 0, :]
            to_pe(V.tensor_copy(rowtot, rank[:, :, BLOCK - 1]))
            from_pe()
            link(V.tensor_scalar(total[:, 1, :], psP[:, 16:16 + R], float(P - 1), None, ALU.add))
            link(V.tensor_copy(total_i[:, 0, :], total[:, 1, :]))
            link(V.tensor_scalar(total_i[:, 1, :], total_i[:, 0, :], 7, None, ALU.arith_shift_right))
            link(V.tensor_copy(total[:, 2, :], total_i[:, 1, :]))
            link(V.tensor_tensor_scan(total[:, 3, :], ones[:, 0:R], total[:, 2, :], 0.0, ALU.mult, ALU.add))
            link(V.tensor_tensor(total[:, 4, :], total[:, 3, :], total[:, 2, :], ALU.subtract))
            link(V.scalar_tensor_tensor(out=total[0:BLOCKS, 5, :], in0=total[0:BLOCKS, 4, :], scalar=float(P),
                                        in1=psP[0:BLOCKS, 0:R], op0=ALU.mult, op1=ALU.add))
            link(V.tensor_scalar(total[0:BLOCKS, 5, :], total[0:BLOCKS, 5, :], -1.0, None, ALU.add))
            ob = total[0:BLOCKS, 5, :].rearrange("b (r a) -> b r a", a=1).broadcast_to([BLOCKS, R, BLOCK])
            link(V.tensor_tensor(rank[:, :, :], rank[:, :, :], ob, ALU.add))
            link(V.tensor_tensor(rank[:, :, :], rank[:, :, :], onehot[:, :, :], ALU.mult))
            link(V.memset(rowp[:, 0:1], 0.0))
            link(V.tensor_reduce(rowp[:, 1:P], rank[:, :, :].rearrange("b r j -> b j r"), AX_X, ALU.add))
            link(V.tensor_copy(rowp_i[:, 0, :], rowp[:, :]))
            link(V.tensor_scalar(rowp_i[:, 1, :], rowp_i[:, 0, :], P - 1, None, ALU.bitwise_and))
            link(V.tensor_scalar(rowp_i[:, 2, :], rowp_i[:, 0, :], 7, None, ALU.arith_shift_right))
            link(V.tensor_copy(rowpf[:, 0, :], rowp_i[:, 1, :]))
            link(V.tensor_copy(rowpf[:, 1, :], rowp_i[:, 2, :]))
            link(V.tensor_scalar(rowx[:, :], rowt[:, :], float(R), float(BIG), ALU.is_ge, ALU.mult))
            link(V.tensor_tensor(rowpf[:, 1, :], rowpf[:, 1, :], rowx[:, :], ALU.add))
            link(V.memset(rowpf[:, 1, 0:1], float(BIG)))

            for i, (row, col) in enumerate(((rowd, cold), (rowe, cole), (rows, cols_), (rowk, colk),
                                            (rowpf[:, 0, :], coll), (rowpf[:, 1, :], colq),
                                            (rowg, gidx[:, TILES:COLS]), (rowp, midx), (rowo, oidx))):
                if i == 0:
                    to_pe(V.tensor_copy(rank[0:1, 0, 0:1], rowd[0:1, 0:1]))
                from_pe()
                V.tensor_copy(col if i == 6 else col[:, :], turned_rows[i % 2][:, 0:BLOCKS]).then_inc(s_pv, 1)

            for b in range(BLOCKS):
                if b >= 2:
                    dve.wait_ge(s_perm, b - 1)
                i = b % 2
                V.tensor_scalar(lanes[:, i, :], iota_f[:, :], coll[:, b:b + 1], None, ALU.is_equal)
                V.tensor_scalar(tiles2[:, i, 0, :], iota_f[:, 0:TILES], colq[:, b:b + 1], cols_[:, b:b + 1],
                                ALU.is_equal, ALU.mult)
                V.tensor_scalar(tiles2[:, i, 1, :], iota_f[:, 0:TILES], colq[:, b:b + 1], colk[:, b:b + 1],
                                ALU.is_equal, ALU.mult).then_inc(s_lane, 1)
            dve.wait_ge(s_perm, BLOCKS)
            link(V.tensor_copy(gidx[:, 0:TILES], psR[:, 0:TILES]))
            to_pe(V.tensor_copy(keyc[:, :], psR[:, TILES:2 * TILES]))

            ty = tile_type
            link(V.memset(ty[:, 0, :], 0.0))
            for r in range(R - 1):
                link(V.tensor_scalar(ty[:, 1, :], iota_f[0:1, 0:TILES], total[0:1, 3, r:r + 1], None, ALU.is_ge))
                link(V.tensor_tensor(ty[:, 0, :], ty[:, 0, :], ty[:, 1, :], ALU.add))
            link(V.tensor_copy(tile_type_i[:, :], ty[:, 0, :]))

            from_pe()
            link(V.tensor_copy(keyr[:, :], psP[0:TILES, 0:P]))
            link(V.memset(same[:, :], 0.0))
            link(V.tensor_tensor(same[:, 1:P], keyr[:, 1:P], keyr[:, 0:P - 1], ALU.is_equal))
            link(V.tensor_tensor_scan(runf[:, :], same[:, 0:P], ones[0:TILES, :], 0.0, ALU.mult, ALU.add))
            link(V.tensor_scalar(gate[:, :], same[:, 1:P + 1], -1.0, 1.0, ALU.mult, ALU.add))
            link(V.tensor_tensor(gate[:, :], gate[:, :], runf[:, :], ALU.mult))
            link(V.tensor_tensor_scan(runt[:, ::-1], same[:, P:0:-1], gate[:, ::-1], 0.0, ALU.mult, ALU.add))
            to_pe(V.tensor_copy(same[:, 0:1], same[:, 0:1]))
            from_pe()
            link(V.tensor_copy(ends[:, :, :].rearrange("a c t -> a (c t)"), psR[0:1, 0:4 * TILES]))
            hk, tk, ft, th = (ends[:, c, :] for c in range(4))
            T = TILES
            lr = link_row
            link(V.memset(lr[:, :, :], 0.0))
            joined, whole, fa, fc, fwd, bwd = (lr[:, c, :] for c in range(6))
            link(V.tensor_tensor(joined[:, 1:T], hk[:, 1:T], tk[:, 0:T - 1], ALU.is_equal))
            link(V.tensor_tensor(whole[:, 0:T], hk, tk, ALU.is_equal))
            link(V.tensor_tensor(fa[:, 1:T], joined[:, 1:T], whole[:, 0:T - 1], ALU.mult))
            link(V.tensor_tensor(fc[:, 1:T], joined[:, 1:T], ft[:, 0:T - 1], ALU.mult))
            link(V.tensor_tensor_scan(fwd[:, 0:T], fa[:, 0:T], fc[:, 0:T], 0.0, ALU.mult, ALU.add))
            link(V.tensor_tensor(fa[:, 0:T - 1], joined[:, 1:T], whole[:, 1:T], ALU.mult))
            link(V.tensor_tensor(fc[:, 0:T - 1], joined[:, 1:T], th[:, 1:T], ALU.mult))
            link(V.memset(fa[:, T - 1:T], 0.0))
            link(V.memset(fc[:, T - 1:T], 0.0))
            link(V.tensor_tensor_scan(bwd[:, 0:T][:, ::-1], fa[:, 0:T][:, ::-1], fc[:, 0:T][:, ::-1], 0.0,
                                      ALU.mult, ALU.add))
            to_pe(V.tensor_copy(ty[:, 1, :], ty[:, 1, :]))
            from_pe()
            link(V.tensor_copy(carryc[:, :], psP[0:TILES, 0:2]))
            for key_col, c in ((0, 0), (P - 1, 1)):
                link(V.tensor_scalar(gate[:, :], keyr[:, :], keyr[:, key_col:key_col + 1], carryc[:, c:c + 1],
                                     ALU.is_equal, ALU.mult))
                link(V.tensor_tensor(runt[:, :], runt[:, :], gate[:, :], ALU.add))
            link(V.tensor_scalar(runt[:, :], runt[:, :], 1.0, None, ALU.max))
            to_pe(V.reciprocal(runf[:, :], runt[:, :]))
            from_pe()
            link(V.tensor_copy(wcol[:, :], psP[:, 0:TILES]))

            from_pe()
            link(V.tensor_copy(need[:, 0, :], psR[0:1, 0:BLOCKS]))
            link(V.tensor_copy(need_i[:, 0, :], need[:, 0, :]))
            link(V.tensor_scalar(need_i[:, 1, :], need_i[:, 0, :], 9, None, ALU.arith_shift_right))
            link(V.tensor_scalar(need[:, 0, :], need[:, 0, :], float(LASTROW), None, ALU.is_ge))
            link(V.tensor_copy(need[:, 1, :], need_i[:, 1, :]))
            link(V.tensor_tensor(need[:, 1, :], need[:, 1, :], need[:, 0, :], ALU.add))
            link(V.tensor_scalar(need[:, 1, :], need[:, 1, :], 1.0, float(STEPS), ALU.add, ALU.min))
            V.tensor_copy(need_i[:, 1, :], need[:, 1, :]).then_inc(s_prep, 1)

            def bn(st, tiles):
                u = st.slot
                for t in tiles:
                    if t == 0:
                        dve.wait_ge(x_in[u], st.use(16, 16))
                    if t == DENSE:
                        dve.wait_ge(g_in[u], st.use(16 * EDGE, 16 * EDGE))
                    tile = xin[u][:, t, :] if t < DENSE else xg[u][:, t - DENSE, :]
                    ins = V.bn_stats(raw[:, t, :], tile)
                return ins

            def aggregate(st):
                n = st.tiles(st.kind)
                for t in range(n):
                    ins = V.bn_aggr(mv[:, t, :], raw[:, t, :])
                ins.then_inc(stats, 1)

            def scales(st):
                u, n = st.slot, st.tiles(st.kind)
                dve.wait_ge(std_ready, st.lin(1, 1))
                V.reciprocal(rstd[u][:, 0:n], std[:, 0:n]).then_inc(inv_ready, 1)
                dve.wait_ge(inv_ready, st.lin(1, 1))
                ins = V.scalar_tensor_tensor(out=nmean[u][:, 0:n], in0=mv[:, 0:n, 0], scalar=-1.0,
                                             in1=rstd[u][:, 0:n], op0=ALU.mult, op1=ALU.mult)
                if st.kind == AGG:
                    ins.then_inc(nm_ready, 1)
                    dve.wait_ge(nm_ready, st.lin(1, 1 - AGG0))
                    V.memset(rstd[u][0:1, DENSE:DENSE + EDGE], 0.0)
                    ins = V.memset(nmean[u][0:1, DENSE:DENSE + EDGE], 0.0)
                ins.then_inc(ln_ready, 1)

            def select(st):
                u = st.slot
                dve.wait_ge(spread, st.lin(1, 1 - AGG0))
                b0 = st.lin(EDGE, -EDGE * AGG0)
                d = cold[:, bass.ds(b0, EDGE)].rearrange("p (k a) -> p k a", a=1).broadcast_to([P, EDGE, P])
                V.tensor_tensor(smat[u][:, :, :], psR[:, 0:EDGE * P].rearrange("p (k e) -> p k e", k=EDGE), d,
                                ALU.is_equal).then_inc(s_ready, 1)

            def finish(st, j):
                pos, pair, edge, v = j
                u = st.slot
                dve.wait_ge(prods, st.job(pos, 1))
                if pair is not None:
                    if pair == 0 and not (st.turn is None and st.base < UNROLL):
                        dve.wait_ge(x_out[u], st.use(16, 0))
                    V.scalar_tensor_tensor(out=xout[u][:, 2 * pair:2 * pair + 2, :], in0=psO[v][:, :, :],
                                           scalar=0.0, in1=xin[u][:, 2 * pair:2 * pair + 2, :],
                                           op0=ALU.max, op1=ALU.add).then_inc(fin, 1)
                elif st.kind == MSG:
                    if edge == 0 and not (st.turn is None and st.base < UNROLL):
                        dve.wait_ge(m_out[u], st.use(16, 0))
                    V.tensor_scalar(mbuf[u][:, edge, :], psO[v][:, 0, :],
                                    wcol[:, bass.ds(st.lin(EDGE, edge), 1)], None, ALU.mult).then_inc(fin, 1)
                else:
                    nxt = st if edge + 1 < EDGE else st.after(1)
                    k = (edge + 1) % EDGE
                    if not (st.turn is None and st.base == ROOT0 - 1 and edge == EDGE - 1):
                        if k == 0:
                            dve.wait_ge(m_in[nxt.slot], nxt.use(16 * EDGE, 16 * EDGE, AGG0))
                        V.tensor_copy(mbuf[nxt.slot][0:1, k, :], psO[v][0:1, 0, :]).then_inc(carry, 1)
                    V.scalar_tensor_tensor(out=orow[:, bass.ds(st.lin(EDGE, edge - EDGE * AGG0), 1), :]
                                           .rearrange("p a f -> p (a f)"), in0=psO[v][:, 0, :],
                                           scalar=0.0, in1=xg[u][:, edge, :],
                                           op0=ALU.max, op1=ALU.add).then_inc(fin, 1)

            def body(st):
                last = st.turn is None and st.base == STEPS - 1
                nxt = st.after(1)
                n = nxt.tiles(nxt.kind)
                jobs = st.jobs()
                if st.kind == AGG:
                    select(st)
                if st.turn is None and st.base == AGG0:
                    dve.wait_ge(m_in[st.slot], 16 * EDGE)
                    V.memset(mbuf[st.slot][0:1, 0, :], 0.0).then_inc(carry, 1)
                if not last:
                    ins = bn(nxt, range(0, DENSE))
                    if len(jobs) > PAIRS:
                        finish(st, jobs[0])
                        if n > DENSE:
                            ins = bn(nxt, range(DENSE, n))
                    ins.then_inc(bn_raw, 1)
                    dve.wait_ge(bn_raw, nxt.lin(1, 1))
                finish(st, jobs[1 if len(jobs) > PAIRS and not last else 0])
                if not last:
                    aggregate(nxt)
                if len(jobs) > PAIRS:
                    finish(st, jobs[2])
                if not last:
                    scales(nxt)
                for j in jobs[3 if len(jobs) > PAIRS else 1:]:
                    finish(st, j)

            bn(Step(pl, 0), range(0, DENSE + EDGE)).then_inc(bn_raw, 1)
            dve.wait_ge(bn_raw, 1)
            aggregate(Step(pl, 0))
            scales(Step(pl, 0))
            run_steps(dve, pl, body)

        @block.tensor
        def _(pe):
            MM = nc.tensor.matmul
            ready = [0]

            def from_dve():
                ready[0] += 1
                pe.wait_ge(s_pv, ready[0])

            pe.wait_ge(s_pool, 9)
            from_dve()
            rowtot = total[0:BLOCKS, 0, :]
            MM(psP[0:BLOCKS, 0:R], upper[0:BLOCKS, 0:BLOCKS], rowtot, start=True, stop=True)
            MM(psP[:, 16:16 + R], ones[0:BLOCKS, :], rowtot, start=True, stop=True).then_inc(s_pp, 1)
            from_dve()
            for i, row in enumerate((rowd, rowe, rows, rowk, rowpf[:, 0, :], rowpf[:, 1, :], rowg, rowp, rowo)):
                if i >= 2:
                    from_dve()
                nc.tensor.transpose(turned_rows[i % 2][:, 0:BLOCKS], row[:, 0:P], ident[0:BLOCKS, 0:BLOCKS]).then_inc(s_pp, 1)
            from_dve()
            from_dve()
            for b in range(BLOCKS):
                pe.wait_ge(s_lane, b + 1)
                i = b % 2
                MM(psR[:, 0:2 * TILES], lanes[:, i, :], tiles2[:, i, :, :].rearrange("p a q -> p (a q)"),
                   start=(b == 0), stop=(b == BLOCKS - 1)).then_inc(s_perm, 1)
            from_dve()
            nc.tensor.transpose(psP[0:TILES, 0:P], keyc[:, :], ident[:, :]).then_inc(s_pp, 1)
            from_dve()
            for c, col in enumerate((keyr[:, 0:1], keyr[:, P - 1:P], runf[:, P - 1:P], runt[:, 0:1])):
                ins = nc.tensor.transpose(psR[0:1, c * TILES:(c + 1) * TILES], col, ident[0:TILES, 0:TILES])
            ins.then_inc(s_pp, 1)
            from_dve()
            for c in range(2):
                ins = MM(psP[0:TILES, c:c + 1], link_row[:, 4 + c, 0:TILES], ones[0:1, 0:1], start=True, stop=True)
            ins.then_inc(s_pp, 1)
            from_dve()
            nc.tensor.transpose(psP[:, 0:TILES], runf[:, :], ident[0:TILES, 0:TILES]).then_inc(s_pp, 1)
            nc.tensor.transpose(psR[0:1, 0:BLOCKS], rowd[:, P - 1:P],
                                ident[0:BLOCKS, 0:BLOCKS]).then_inc(s_pp, 1)
            pe.wait_ge(s_prep, 1)
            pe.wait_ge(s_w, 16 * 2 * KC)

            def turn(st, j):
                pos, pair, edge, v = j
                pe.wait_ge(normed, st.job(pos, 1))
                if not (st.turn is None and st.base == 0 and pos < 2):
                    pe.wait_ge(hT_ready, st.job(pos, -1))
                for t in range(1 if pair is None else 2):
                    for k in range(KC):
                        ins = nc.tensor.transpose(psT[v][:, t * KC + k, :], h[v][:, t, k * P:(k + 1) * P], ident[:, :])
                ins.then_inc(turned, 1)

            def spread_dst(st):
                if not (st.turn is None and st.base == AGG0):
                    pe.wait_ge(s_ready, st.lin(1, -AGG0))
                pe.wait_ge(e_slot, st.lin(1, 1 - AGG0))
                for k in range(EDGE):
                    e = eslot[st.slot][:, k:k + 1]
                    ins = nc.tensor.transpose(psR[:, k * P:(k + 1) * P], e.broadcast_to([P, P]), ident[:, :])
                ins.then_inc(spread, 1)

            def product(st, j):
                pos, pair, edge, v = j
                if pair is None and st.kind == MSG:
                    r = nc.tensor.value_load(tile_type_i[0:1, bass.ds(st.lin(EDGE, edge), 1)], min_val=0, max_val=R - 1)
                pe.wait_ge(hT_ready, st.job(pos, 1))
                if not (st.turn is None and st.base == 0 and pos < 2):
                    pe.wait_ge(fin, st.job(pos, -1))
                if pair is not None:
                    MM(psO[v][:, :, :].rearrange("p a f -> p (a f)"), ones3[:, :],
                       bias_rows[:, :, :].rearrange("p a f -> p (a f)"), start=True, stop=False, skip_group_check=True)
                    for t in range(2):
                        for k in range(KC):
                            ins = MM(psO[v][:, t, :], hT[v][:, t * KC + k, :], wr_sb[:, k, :], start=False,
                                     stop=(t == 1 and k == KC - 1), skip_group_check=True)
                elif st.kind == MSG:
                    for k in range(KC):
                        ins = MM(psO[v][:, 0, :], hT[v][:, k, :], w_sb[:, bass.ds(r * F + k * R * F, F)],
                                 start=(k == 0), stop=(k == KC - 1))
                else:
                    u = st.slot
                    MM(psO[v][:, 0, :], ones3_agg[:, :], bias_rows[:, 0, :], start=True, stop=False)
                    for k in range(KC):
                        MM(psO[v][:, 0, :], hT[v][:, k, :], wr_sb[:, k, :], start=False, stop=False)
                    if edge == 0:
                        pe.wait_ge(s_ready, st.lin(1, 1 - AGG0))
                        pe.wait_ge(m_in[u], st.use(16 * EDGE, 16 * EDGE, AGG0))
                    pe.wait_ge(carry, st.lin(EDGE, edge + 1 - EDGE * AGG0))
                    ins = MM(psO[v][:, 0, :], smat[u][:, edge, :], mbuf[u][:, edge, :], start=False, stop=True)
                ins.then_inc(prods, 1)

            def body(st):
                jobs = st.jobs()
                turn(st, jobs[0])
                if not (st.turn is None and st.base == 0):
                    prev = st.after(-1)
                    product(prev, prev.jobs()[-1])
                if st.kind == AGG:
                    spread_dst(st)
                for a, b in zip(jobs[1:], jobs[:-1]):
                    turn(st, a)
                    product(st, b)

            run_steps(pe, pl, body)
            last = Step(pl, STEPS - 1)
            product(last, last.jobs()[-1])


_INS = ["x", "src", "dst", "edge_type_8", "L0_gnn_W", "L0_gnn_W_root", "L0_gnn_bias"]


def kernel(**inputs):
    import numpy as _np
    import concourse.bacc as _bacc
    from concourse import mybir as _mybir
    from concourse.bass_utils import run_bass_kernel_spmd as _run

    nc = _bacc.Bacc("TRN2", target_bir_lowering=False, num_devices=1)
    arrays, args = {}, []
    for name in _INS:
        a = _np.ascontiguousarray(inputs[name])
        arrays[f"in_{name}_dram"] = a
        args.append(nc.dram_tensor(f"in_{name}_dram", a.shape, _mybir.dt.from_np(a.dtype), kind="ExternalInput").ap())
    out = nc.dram_tensor("out_dram", inputs["x"].shape, _mybir.dt.float32, kind="ExternalOutput").ap()
    build(nc, *args, out)
    r = _run(nc, [arrays], core_ids=[0])
    return r.results[0]["out_dram"]
```

```python
from contextlib import ExitStack

import concourse.bass as bass
from concourse import mybir

F32 = mybir.dt.float32
BF16 = mybir.dt.bfloat16
I32 = mybir.dt.int32
ALU = mybir.AluOpType
ACT = mybir.ActivationFunctionType
AX_X = mybir.AxisListType.X

P = 128
UNROLL = 4
DENSE, PAIRS = 4, 2
SLOTS = 4
EDGE = 3
BIG = 1 << 20
EPS = 1e-05
MSG, AGG, ROOT = range(3)


def cdiv(a, b):
    return -(-a // b)


def wait(eng, sem, value):
    if not isinstance(value, int) or value > 0:
        eng.wait_ge(sem, value)


class Plan:

    def __init__(self, n, f, e, r):
        self.N, self.F, self.E, self.R = n, f, e, r
        self.GROUP = P * DENSE
        self.STEPS = cdiv(n, self.GROUP)
        self.BLOCK = P - 1
        self.BLOCKS = cdiv(e, self.BLOCK)
        self.TILES = (e + r * (P - 1)) // P
        self.MSG_STEPS = cdiv(self.TILES, EDGE)
        self.AGG_STEPS = cdiv(self.BLOCKS, EDGE)
        assert self.TILES == EDGE * self.MSG_STEPS and self.BLOCKS == EDGE * self.AGG_STEPS
        self.AGG0 = self.MSG_STEPS
        self.ROOT0 = self.AGG0 + self.AGG_STEPS
        assert self.ROOT0 < self.STEPS

    def kind(self, s):
        return MSG if s < self.AGG0 else AGG if s < self.ROOT0 else ROOT


class Step:

    def __init__(self, plan, base, turn=None):
        self.plan, self.base, self.turn = plan, base, turn
        self.slot = base % UNROLL
        self.kind = plan.kind(base)
        self.next_kind = plan.kind(base + 1)

    def lin(self, a, c):
        return a * self.base + c if self.turn is None else self.turn * (a * UNROLL) + (a * self.base + c)

    def use(self, scale, c, first=0):
        n = (self.base - first) // UNROLL
        return scale * n + c if self.turn is None else self.turn * scale + (scale * n + c)

    def jobs(self):
        order = [(0, None), (1, None)] if self.kind == ROOT else [(0, None), (None, 0), (1, None), (None, 1), (None, 2)]
        first = Step(self.plan, self.base)
        return [(pos, pair, edge, first.job(pos) % SLOTS) for pos, (pair, edge) in enumerate(order)]

    def job(self, pos, c=0):
        if self.kind == ROOT:
            root0 = self.plan.ROOT0
            return self.lin(PAIRS, (EDGE + PAIRS) * root0 - PAIRS * root0 + pos + c)
        return self.lin(EDGE + PAIRS, pos + c)

    def tiles(self, kind):
        return DENSE if kind == ROOT else DENSE + EDGE

    def after(self, k):
        return Step(self.plan, self.base + k, self.turn)


def run_steps(eng, plan, body, ends=None):
    def peeled(a, b):
        for s in range(a, b):
            body(Step(plan, s))

    def looped(a, b):
        turns = (b - a) // UNROLL
        if turns < 2:
            return peeled(a, b)
        with eng.Fori(0, turns) as turn:
            for c in range(UNROLL):
                body(Step(plan, a + c, turn))
        peeled(a + UNROLL * turns, b)

    a, b, c = plan.AGG0, plan.ROOT0, plan.STEPS
    first = a % UNROLL or UNROLL
    peeled(0, first)
    looped(first, a - UNROLL)
    peeled(a - UNROLL, a + UNROLL)
    looped(a + UNROLL, b - UNROLL)
    peeled(b - UNROLL, b)
    if ends == b:
        return
    peeled(b, b + UNROLL)
    looped(b + UNROLL, c - UNROLL)
    peeled(c - UNROLL, c)


def run_blocks(eng, blocks, body):
    first = blocks % UNROLL or UNROLL
    turns = (blocks - first) // UNROLL - 1
    for b in range(first):
        body(b, b % UNROLL)
    with eng.Fori(0, turns) as turn:
        for c in range(UNROLL):
            body(turn * UNROLL + (first + c), (first + c) % UNROLL)
    for b in range(first + turns * UNROLL, blocks):
        body(b, b % UNROLL)


def build(nc, x, src, dst, etype, W, W_root, bias, out):
    N, F = x.shape
    R = W.shape[0]
    E = src.shape[0]
    KC = F // P
    pl = Plan(N, F, E, R)
    BLOCK, BLOCKS, TILES, STEPS = pl.BLOCK, pl.BLOCKS, pl.TILES, pl.STEPS
    AGG0, ROOT0 = pl.AGG0, pl.ROOT0
    COLS = TILES + BLOCKS
    TEVEN = TILES + TILES % 2
    LASTROW = N - pl.GROUP
    PAD = N + 10000
    assert F == 2 * P and PAD + 1 < (1 << 16) and TILES <= P and BLOCKS <= P

    ctx = ExitStack()
    with ctx:
        def sb(name, shape, dt=F32):
            return ctx.enter_context(nc.sbuf_tensor(name, shape, dt))

        early = ExitStack()

        def pre(name, shape, dt=F32):
            return early.enter_context(nc.sbuf_tensor(name, shape, dt))

        def ps(name, shape, dt=F32):
            return ctx.enter_context(nc.psum_tensor(name, shape, dt))

        def sem(name):
            return ctx.enter_context(nc.semaphore(name))

        msgs = nc.dram_tensor("msgs", [TILES * P, F], F32, kind="Internal").ap()

        w_sb = sb("w_sb", [P, KC * R * F])
        wr_sb = sb("wr_sb", [P, KC, F])
        ident = sb("ident", [P, P])
        eps = sb("eps", [P, 1])
        bias_rows = sb("bias_rows", [P, 2, F], BF16)
        ones3 = sb("ones3", [P, P], BF16)
        ones3_agg = sb("ones3_agg", [P, P], BF16)
        cold = sb("cold", [P, BLOCKS])
        cole = sb("cole", [P, BLOCKS])
        gidx = sb("gidx", [P, COLS], I32)
        midx = sb("midx", [P, BLOCKS], I32)
        oidx = sb("oidx", [P, BLOCKS], I32)
        wcol = sb("wcol", [P, TILES])
        tile_type_i = sb("tile_type_i", [1, TILES], I32)
        need_i = sb("need_i", [1, 2, BLOCKS], I32)
        xin = [sb(f"xin{u}", [P, DENSE, F]) for u in range(UNROLL)]
        xout = [sb(f"xout{u}", [P, DENSE, F]) for u in range(UNROLL)]
        xg = [sb(f"xg{u}", [P, EDGE, F]) for u in range(UNROLL)]
        mbuf = [sb(f"mbuf{u}", [P, EDGE, F]) for u in range(UNROLL)]
        smat = [sb(f"smat{u}", [P, EDGE, P]) for u in range(UNROLL)]
        gslot = [sb(f"gslot{u}", [P, EDGE], I32) for u in range(UNROLL)]
        mslot = [sb(f"mslot{u}", [P, EDGE], I32) for u in range(UNROLL)]
        eslot = [sb(f"eslot{u}", [P, EDGE]) for u in range(UNROLL)]
        raw = sb("raw", [P, DENSE + EDGE, 6])
        mv = sb("mv", [P, DENSE + EDGE, 2])
        std = sb("std", [P, DENSE + EDGE])
        rstd = [sb(f"rstd{u}", [P, DENSE + EDGE]) for u in range(UNROLL)]
        nmean = [sb(f"nmean{u}", [P, DENSE + EDGE]) for u in range(UNROLL)]
        h = [sb(f"h{v}", [P, 2, F]) for v in range(SLOTS)]
        hT = [sb(f"hT{v}", [P, 2 * KC, P]) for v in range(SLOTS)]
        upper = pre("upper", [P, P])
        ones = pre("ones", [P, P])
        iota_i = pre("iota_i", [P, P], I32)
        iota_f = pre("iota_f", [P, P])
        bias3 = pre("bias3", [3, F])
        bpart = pre("bpart", [3, 3, F], BF16)
        bres = pre("bres", [3, F])
        rowd_i = pre("rowd_i", [BLOCKS, P + 1], I32)
        rows_i = pre("rows_i", [BLOCKS, P], I32)
        rowt_i = pre("rowt_i", [BLOCKS, P], I32)
        rowd = pre("rowd", [BLOCKS, P + 1])
        rows = pre("rows", [BLOCKS, P])
        rowt = pre("rowt", [BLOCKS, P])
        rowe = pre("rowe", [BLOCKS, P])
        rowx = pre("rowx", [BLOCKS, P])
        rowo = pre("rowo", [BLOCKS, P])
        rowg = pre("rowg", [BLOCKS, P])
        rowk = pre("rowk", [BLOCKS, P])
        onehot = pre("onehot", [BLOCKS, R, BLOCK])
        notfirst = pre("notfirst", [BLOCKS, R, BLOCK])
        rank = pre("rank", [BLOCKS, R, BLOCK])
        types_i = pre("types_i", [P, R], I32)
        types = pre("types", [P, R])
        total = pre("total", [P, 8, R])
        total_i = pre("total_i", [P, 2, R], I32)
        rowp = pre("rowp", [BLOCKS, P])
        rowp_i = pre("rowp_i", [BLOCKS, 3, P], I32)
        rowpf = pre("rowpf", [BLOCKS, 2, P])
        cols_ = pre("cols_", [P, BLOCKS])
        colk = pre("colk", [P, BLOCKS])
        coll = pre("coll", [P, BLOCKS])
        colq = pre("colq", [P, BLOCKS])
        lanes = pre("lanes", [P, UNROLL, P])
        tiles2 = pre("tiles2", [P, UNROLL, 2, TEVEN])
        keyc = pre("keyc", [P, TILES])
        keyr = pre("keyr", [TILES, P])
        same = pre("same", [TILES, P + 1])
        runf = pre("runf", [TILES, P])
        runt = pre("runt", [TILES, P])
        gate = pre("gate", [TILES, P])
        ends = pre("ends", [1, 4, TILES])
        link_row = pre("link_row", [1, 6, TILES + 1])
        carryc = pre("carryc", [TILES, 2])
        tile_type = pre("tile_type", [1, 2, TILES])
        need = pre("need", [1, 2, BLOCKS])
        early.close()
        orow = sb("orow", [P, BLOCKS, F])

        psT = [ps(f"psT{v}", [P, 2 * KC, P]) for v in range(2)]
        psO = [ps(f"psO{v}", [P, 2, F]) for v in range(SLOTS)]
        psR = ps("psR", [P, 512])
        psP = ps("psP", [P, 512])
        turned_rows = (psP, psR)

        s_w = sem("s_w")
        s_bias = sem("s_bias")
        s_list = sem("s_list")
        s_fill = sem("s_fill")
        s_pool = sem("s_pool")
        s_c = sem("s_c")
        s_pp = sem("s_pp")
        s_pv = sem("s_pv")
        s_lane = sem("s_lane")
        s_tile = sem("s_tile")
        s_perm = sem("s_perm")
        s_prep = sem("s_prep")
        s_eps = sem("s_eps")
        x_in = [sem(f"x_in{u}") for u in range(UNROLL)]
        x_out = [sem(f"x_out{u}") for u in range(UNROLL)]
        g_in = [sem(f"g_in{u}") for u in range(UNROLL)]
        m_in = [sem(f"m_in{u}") for u in range(UNROLL)]
        m_out = [sem(f"m_out{u}") for u in range(UNROLL)]
        idx_ready = sem("idx_ready")
        fetches = sem("fetches")
        e_slot = sem("e_slot")
        bn_raw = sem("bn_raw")
        stats = sem("stats")
        std_ready = sem("std_ready")
        inv_ready = sem("inv_ready")
        nm_ready = sem("nm_ready")
        ln_ready = sem("ln_ready")
        normed = sem("normed")
        turned = sem("turned")
        hT_ready = sem("hT_ready")
        prods = sem("prods")
        fin = sem("fin")
        spread = sem("spread")
        s_ready = sem("s_ready")
        carry = sem("carry")
        rows_out = sem("rows_out")
        s_scat = sem("s_scat")

        block = ctx.enter_context(nc.Block())

        def node_rows(t, st):
            if st.turn is None:
                r0 = min(st.base * pl.GROUP, LASTROW)
                v = t[r0:r0 + pl.GROUP, :]
            else:
                v = t[bass.ds(st.lin(pl.GROUP, 0), pl.GROUP), :]
            return v.rearrange("(p j) f -> p (j f)", p=P)

        def flat(t):
            return t[:, :, :].rearrange("p a b -> p (a b)")

        @block.sync
        def _(sp):
            LAST = BLOCKS - 1
            TAIL = E - (BLOCK * LAST - 1)
            sp.wait_ge(s_fill, 3)
            n_list = 0
            for row, lst, width in ((rowd_i, dst, P + 1), (rows_i, src, P), (rowt_i, etype, P)):
                body = bass.AP(tensor=lst.tensor, offset=BLOCK - 1, ap=[[BLOCK, LAST - 1], [1, width]])
                sp.dma_start(row[1:LAST, 0:width], body).then_inc(s_list, 16)
                sp.dma_start(row[0:1, 1:width],
                             lst[0:width - 1].rearrange("(a c) -> a c", a=1)).then_inc(s_list, 16)
                sp.dma_start(row[LAST:LAST + 1, 0:TAIL],
                             lst[E - TAIL:E].rearrange("(a c) -> a c", a=1)).then_inc(s_list, 16)
            b1 = bias.rearrange("(a c) -> a c", a=1)
            for j in range(3):
                sp.dma_start(bias3[j:j + 1, :], b1).then_inc(s_bias, 16)
            for u in range(UNROLL):
                sp.dma_start(flat(xin[u]), node_rows(x, Step(pl, u))).then_inc(x_in[u], 16)
            for k in range(KC):
                sp.dma_start(wr_sb[:, k, :], W_root[k * P:(k + 1) * P, :]).then_inc(s_w, 16)
                sp.dma_start(w_sb[:, k * R * F:(k + 1) * R * F].rearrange("p (r o) -> p r o", r=R),
                             W[:, k * P:(k + 1) * P, :].rearrange("r p o -> p r o")).then_inc(s_w, 16)

            def relay(st):
                sp.wait_ge(x_out[st.slot], st.use(16, 16))
                sp.sem_inc(rows_out, 1)

            def body(st):
                u = st.slot
                pos = 1 if st.kind == ROOT else 2
                sp.wait_ge(fin, st.job(pos, 1))
                last = st.turn is None and st.base == STEPS - 1
                if last:
                    relay(st.after(-1))
                sp.dma_start(node_rows(out, st), flat(xout[u])).then_inc(x_out[u], 16)
                if st.turn is not None or st.base + UNROLL < STEPS:
                    sp.dma_start(flat(xin[u]), node_rows(x, st.after(UNROLL))).then_inc(x_in[u], 16)
                if st.kind == MSG:
                    sp.wait_ge(fin, st.job(4, 1))
                    sp.dma_start(msgs[bass.ds(st.lin(EDGE * P, 0), EDGE * P), :].rearrange("(k p) f -> p k f", k=EDGE),
                                 mbuf[u][:, :, :]).then_inc(m_out[u], 16)
                if not last and not (st.turn is None and st.base == 0):
                    relay(st.after(-1))

            run_steps(sp, pl, body)
            relay(Step(pl, STEPS - 1))

        @block.gpsimd
        def _(pool):
            nc.gpsimd.memset(rowd_i[:, :], PAD).then_inc(s_fill, 1)
            nc.gpsimd.memset(rows_i[:, :], 0).then_inc(s_fill, 1)
            nc.gpsimd.memset(rowt_i[:, :], R).then_inc(s_fill, 1)
            nc.gpsimd.iota(iota_i[:, :], [[1, P]], base=0, channel_multiplier=0).then_inc(s_pool, 1)
            nc.gpsimd.iota(types_i[:, :], [[1, R]], base=0, channel_multiplier=0).then_inc(s_pool, 1)
            nc.gpsimd.memset(ident[:, :], 0.0).then_inc(s_pool, 1)
            nc.gpsimd.memset(upper[:, :], 0.0).then_inc(s_pool, 1)
            nc.gpsimd.memset(ones[:, :], 1.0).then_inc(s_pool, 1)
            nc.gpsimd.memset(notfirst[:, :, :], 1.0).then_inc(s_pool, 1)
            nc.gpsimd.memset(eps[:, :], EPS).then_inc(s_eps, 1)
            pool.wait_ge(s_pool, 6)
            nc.gpsimd.affine_select(out=ident[:, :], in_=ident[:, :], compare_op=ALU.not_equal, fill=1.0,
                                    base=0, pattern=[[-1, P]], channel_multiplier=1).then_inc(s_pool, 1)
            nc.gpsimd.affine_select(out=upper[:, :], in_=upper[:, :], compare_op=ALU.is_ge, fill=1.0,
                                    base=0, pattern=[[-1, P]], channel_multiplier=1).then_inc(s_pool, 1)
            nc.gpsimd.memset(notfirst[:, :, 0:1], 0.0).then_inc(s_pool, 1)
            pool.wait_ge(s_pv, 7)
            for b in range(BLOCKS):
                wait(pool, s_perm, b - UNROLL + 1)
                nc.gpsimd.tensor_scalar(lanes[:, b % UNROLL, :], iota_f[:, :], coll[:, b:b + 1], None,
                                        ALU.is_equal).then_inc(s_lane, 1)

            def slot_indices(slot, cols):
                nc.gpsimd.tensor_copy(slot[:, :], cols).then_inc(idx_ready, 1)

            def gather_x(st):
                u = st.slot
                for k in range(EDGE):
                    nc.gpsimd.indirect_dma_start(
                        out=xg[u][:, k, :], out_offset=None, in_=x[:, :],
                        in_offset=bass.IndirectOffsetOnAxis(ap=gslot[u][:, k:k + 1], axis=0)).then_inc(g_in[u], 16)

            def gather_m(st):
                u = st.slot
                for k in range(EDGE):
                    nc.gpsimd.indirect_dma_start(
                        out=mbuf[u][:, k, :], out_offset=None, in_=msgs[:, :],
                        in_offset=bass.IndirectOffsetOnAxis(ap=mslot[u][:, k:k + 1], axis=0)).then_inc(m_in[u], 16)

            def x_copies(st):
                if st.kind == MSG or (st.turn is None and st.base < AGG0 + UNROLL):
                    return st.lin(1, 1)
                return st.lin(2, 2 - 1 - AGG0)

            def m_copies(st):
                if st.turn is None and st.base < AGG0 + UNROLL:
                    return AGG0 + UNROLL + (st.base - AGG0) + 1
                return st.lin(2, 2 - AGG0)

            def fetch_x(st):
                slot_indices(gslot[st.slot], gidx[:, bass.ds(st.lin(EDGE, 0), EDGE)])
                if st.kind == AGG:
                    nc.gpsimd.tensor_copy(eslot[st.slot][:, :],
                                          cole[:, bass.ds(st.lin(EDGE, -EDGE * AGG0), EDGE)]).then_inc(e_slot, 1)
                pool.wait_ge(idx_ready, x_copies(st))
                pool.sem_inc(fetches, 1)
                gather_x(st)

            def fetch_m(st):
                slot_indices(mslot[st.slot], midx[:, bass.ds(st.lin(EDGE, -EDGE * AGG0), EDGE)])
                pool.wait_ge(idx_ready, m_copies(st))
                pool.sem_inc(fetches, 1)
                gather_m(st)

            pool.wait_ge(s_prep, 1)
            for u in range(UNROLL):
                fetch_x(Step(pl, u))

            def body(st):
                if st.kind == ROOT:
                    return
                nxt = st.after(UNROLL)
                if st.turn is None and nxt.base >= ROOT0:
                    return
                pool.wait_ge(fin, st.job(4, 1))
                fetch_x(nxt)
                if st.kind == AGG:
                    fetch_m(nxt)
                elif st.turn is None and st.base == AGG0 - 1:
                    for u in range(UNROLL):
                        pool.wait_ge(m_out[u], Step(pl, AGG0 - UNROLL + (u - AGG0) % UNROLL).use(16, 16))
                    for v in range(UNROLL):
                        fetch_m(Step(pl, AGG0 + v))

            run_steps(pool, pl, body, ends=ROOT0)
            for b in range(BLOCKS):
                if b % EDGE == 0:
                    pool.wait_ge(fin, Step(pl, AGG0 + b // EDGE).job(4, 1))
                steps_needed = nc.gpsimd.value_load(need_i[0:1, 1, b:b + 1], min_val=1, max_val=STEPS)
                pool.wait_ge(rows_out, steps_needed)
                pool.sem_inc(fetches, 1)
                nc.gpsimd.indirect_dma_start(
                    out=out[:, :], out_offset=bass.IndirectOffsetOnAxis(ap=oidx[:, b:b + 1], axis=0),
                    in_=orow[:, b, :], in_offset=None, bounds_check=N - 1, oob_is_err=False).then_inc(s_scat, 16)
            pool.wait_ge(s_scat, 16 * BLOCKS)

        @block.scalar
        def _(act):
            act.wait_ge(s_eps, 1)

            def deviations(st):
                n = st.tiles(st.kind)
                act.wait_ge(stats, st.lin(1, 1))
                nc.scalar.activation(std[:, 0:n], mv[:, 0:n, 1], ACT.Sqrt, bias=eps[:, 0:1]).then_inc(std_ready, 1)

            def norm(st, j):
                pos, pair, edge, v = j
                u = st.slot
                if pos == 0:
                    act.wait_ge(ln_ready, st.lin(1, 1))
                wait(act, turned, st.job(pos, 1 - SLOTS))
                if pair is None:
                    t = DENSE + edge
                    ins = nc.scalar.activation(h[v][:, 0, :], xg[u][:, edge, :], ACT.Relu,
                                               scale=rstd[u][:, t:t + 1], bias=nmean[u][:, t:t + 1])
                else:
                    for c in range(2):
                        t = 2 * pair + c
                        ins = nc.scalar.activation(h[v][:, c, :], xin[u][:, t, :], ACT.Relu,
                                                   scale=rstd[u][:, t:t + 1], bias=nmean[u][:, t:t + 1])
                ins.then_inc(normed, 1)

            def evacuate(st, j):
                pos, pair, edge, v = j
                act.wait_ge(turned, st.job(pos, 1))
                wait(act, prods, st.job(pos, 1 - SLOTS))
                n = KC if pair is None else 2 * KC
                nc.scalar.activation(hT[v][:, 0:n, :], psT[v % 2][:, 0:n, :], ACT.Copy).then_inc(hT_ready, 1)

            def body(st):
                jobs, left = st.jobs(), STEPS if st.turn is not None else STEPS - st.base
                for i, j in enumerate(jobs):
                    evacuate(st, j)
                    if i + 2 < len(jobs):
                        norm(st, jobs[i + 2])
                    elif left > 1:
                        nxt = st.after(1)
                        norm(nxt, nxt.jobs()[i + 2 - len(jobs)])
                if left > 2:
                    deviations(st.after(2))

            for s in range(2):
                deviations(Step(pl, s))
                if s == 0:
                    for j in Step(pl, 0).jobs()[:2]:
                        norm(Step(pl, 0), j)
            run_steps(act, pl, body)

        @block.vector
        def _(dve):
            chain = [0]

            def link(ins):
                chain[0] += 1
                ins.then_inc(s_c, 1)
                dve.wait_ge(s_c, chain[0])

            V = nc.vector
            pe_done = [0]

            def from_pe():
                pe_done[0] += 1
                dve.wait_ge(s_pp, pe_done[0])

            def to_pe(ins):
                ins.then_inc(s_pv, 1)

            dve.wait_ge(s_pool, 9)
            link(V.tensor_copy(iota_f[:, :], iota_i[:, :]))
            link(V.tensor_copy(types[:, :], types_i[:, :]))
            dve.wait_ge(s_bias, 48)
            link(V.memset(bias_rows[:, :, :], 0.0))
            link(V.tensor_copy(bpart[:, 0, :], bias3[:, :]))
            link(V.tensor_tensor(bres[:, :], bias3[:, :], bpart[:, 0, :], ALU.subtract))
            link(V.tensor_copy(bpart[:, 1, :], bres[:, :]))
            link(V.tensor_tensor(bres[:, :], bres[:, :], bpart[:, 1, :], ALU.subtract))
            link(V.tensor_copy(bpart[:, 2, :], bres[:, :]))
            link(V.tensor_scalar(bres[:, :], bpart[:, 0, :], ident[0:3, 0:1], None, ALU.mult))
            for k in (1, 2):
                link(V.scalar_tensor_tensor(out=bres[:, :], in0=bpart[:, k, :], scalar=ident[0:3, k:k + 1],
                                            in1=bres[:, :], op0=ALU.mult, op1=ALU.add))
            for t in range(2):
                link(V.tensor_copy(bias_rows[0:3, t, :], bres[:, :]))
            link(V.memset(ones3[:, :], 0.0))
            link(V.memset(ones3[0:3, :], 1.0))
            link(V.tensor_copy(ones3_agg[:, :], ones3[:, :]))
            link(V.memset(ones3_agg[:, 0:1], 0.0))

            dve.wait_ge(s_list, 16 * 9)
            link(V.tensor_copy(rowd[:, :], rowd_i[:, :]))
            link(V.tensor_copy(rows[:, :], rows_i[:, :]))
            link(V.tensor_copy(rowt[:, :], rowt_i[:, :]))
            link(V.tensor_copy(rowe[:, :], rowd[:, 0:P]))
            link(V.tensor_copy(rowe[:, 0:1], rowd[:, P - 1:P]))
            link(V.tensor_tensor(rowx[:, :], rowd[:, 0:P], rowd[:, 1:P + 1], ALU.is_equal))
            link(V.scalar_tensor_tensor(out=rowo[:, :], in0=rowx[:, :], scalar=float(BIG), in1=rowd[:, 0:P],
                                        op0=ALU.mult, op1=ALU.add))
            link(V.memset(rowo[:, 0:1], float(BIG)))
            link(V.tensor_scalar(rowg[:, :], rowd[:, 0:P], float(N - 1), None, ALU.min))
            link(V.scalar_tensor_tensor(out=rowk[:, :], in0=rowt[:, :], scalar=65536.0, in1=rowd[:, 0:P],
                                        op0=ALU.mult, op1=ALU.add))
            link(V.tensor_scalar(rowk[:, :], rowk[:, :], 1.0, None, ALU.add))

            tb = rowt[:, 1:P].rearrange("b (a j) -> b a j", a=1).broadcast_to([BLOCKS, R, BLOCK])
            yb = types[0:BLOCKS, :].rearrange("b (r a) -> b r a", a=1).broadcast_to([BLOCKS, R, BLOCK])
            link(V.tensor_tensor(onehot[:, :, :], tb, yb, ALU.is_equal))
            link(V.tensor_tensor_scan(flat(rank), flat(notfirst), flat(onehot), 0.0, ALU.mult, ALU.add))
            rowtot = total[0:BLOCKS, 0, :]
            to_pe(V.tensor_copy(rowtot, rank[:, :, BLOCK - 1]))
            from_pe()
            link(V.tensor_scalar(total[:, 1, :], psP[:, 16:16 + R], float(P - 1), None, ALU.add))
            link(V.tensor_copy(total_i[:, 0, :], total[:, 1, :]))
            link(V.tensor_scalar(total_i[:, 1, :], total_i[:, 0, :], 7, None, ALU.arith_shift_right))
            link(V.tensor_copy(total[:, 2, :], total_i[:, 1, :]))
            link(V.tensor_tensor_scan(total[:, 3, :], ones[:, 0:R], total[:, 2, :], 0.0, ALU.mult, ALU.add))
            link(V.tensor_tensor(total[:, 4, :], total[:, 3, :], total[:, 2, :], ALU.subtract))
            link(V.scalar_tensor_tensor(out=total[0:BLOCKS, 5, :], in0=total[0:BLOCKS, 4, :], scalar=float(P),
                                        in1=psP[0:BLOCKS, 0:R], op0=ALU.mult, op1=ALU.add))
            link(V.tensor_scalar(total[0:BLOCKS, 5, :], total[0:BLOCKS, 5, :], -1.0, None, ALU.add))
            ob = total[0:BLOCKS, 5, :].rearrange("b (r a) -> b r a", a=1).broadcast_to([BLOCKS, R, BLOCK])
            link(V.tensor_tensor(rank[:, :, :], rank[:, :, :], ob, ALU.add))
            link(V.tensor_tensor(rank[:, :, :], rank[:, :, :], onehot[:, :, :], ALU.mult))
            link(V.memset(rowp[:, 0:1], 0.0))
            link(V.tensor_reduce(rowp[:, 1:P], rank[:, :, :].rearrange("b r j -> b j r"), AX_X, ALU.add))
            link(V.tensor_copy(rowp_i[:, 0, :], rowp[:, :]))
            link(V.tensor_scalar(rowp_i[:, 1, :], rowp_i[:, 0, :], P - 1, None, ALU.bitwise_and))
            link(V.tensor_scalar(rowp_i[:, 2, :], rowp_i[:, 0, :], 7, None, ALU.arith_shift_right))
            link(V.tensor_copy(rowpf[:, 0, :], rowp_i[:, 1, :]))
            link(V.tensor_copy(rowpf[:, 1, :], rowp_i[:, 2, :]))
            link(V.tensor_scalar(rowx[:, :], rowt[:, :], float(R), float(BIG), ALU.is_ge, ALU.mult))
            link(V.tensor_tensor(rowpf[:, 1, :], rowpf[:, 1, :], rowx[:, :], ALU.add))
            link(V.memset(rowpf[:, 1, 0:1], float(BIG)))

            for i, (row, col) in enumerate(((rowd, cold), (rowe, cole), (rows, cols_), (rowk, colk),
                                            (rowpf[:, 0, :], coll), (rowpf[:, 1, :], colq),
                                            (rowg, gidx[:, TILES:COLS]), (rowp, midx), (rowo, oidx))):
                if i == 0:
                    to_pe(V.tensor_copy(rank[0:1, 0, 0:1], rowd[0:1, 0:1]))
                from_pe()
                V.tensor_copy(col if i == 6 else col[:, :], turned_rows[i % 2][:, 0:BLOCKS]).then_inc(s_pv, 1)

            def one_hot_tiles(b, i):
                wait(dve, s_perm, b - UNROLL + 1)
                for c, val in enumerate((cols_, colk)):
                    ins = V.tensor_scalar(tiles2[:, i, c, :], iota_f[:, 0:TEVEN], colq[:, bass.ds(b, 1)],
                                          val[:, bass.ds(b, 1)], ALU.is_equal, ALU.mult)
                ins.then_inc(s_tile, 1)

            run_blocks(dve, BLOCKS, one_hot_tiles)
            dve.wait_ge(s_perm, BLOCKS)
            link(V.tensor_copy(gidx[:, 0:TILES], psR[:, 0:TILES]))
            to_pe(V.tensor_copy(keyc[:, :], psR[:, TEVEN:TEVEN + TILES]))

            ty = tile_type
            link(V.memset(ty[:, 0, :], 0.0))
            for r in range(R - 1):
                link(V.tensor_scalar(ty[:, 1, :], iota_f[0:1, 0:TILES], total[0:1, 3, r:r + 1], None, ALU.is_ge))
                link(V.tensor_tensor(ty[:, 0, :], ty[:, 0, :], ty[:, 1, :], ALU.add))
            link(V.tensor_copy(tile_type_i[:, :], ty[:, 0, :]))

            from_pe()
            link(V.tensor_copy(keyr[:, :], psP[0:TILES, 0:P]))
            link(V.memset(same[:, :], 0.0))
            link(V.tensor_tensor(same[:, 1:P], keyr[:, 1:P], keyr[:, 0:P - 1], ALU.is_equal))
            link(V.tensor_tensor_scan(runf[:, :], same[:, 0:P], ones[0:TILES, :], 0.0, ALU.mult, ALU.add))
            link(V.tensor_scalar(gate[:, :], same[:, 1:P + 1], -1.0, 1.0, ALU.mult, ALU.add))
            link(V.tensor_tensor(gate[:, :], gate[:, :], runf[:, :], ALU.mult))
            link(V.tensor_tensor_scan(runt[:, ::-1], same[:, P:0:-1], gate[:, ::-1], 0.0, ALU.mult, ALU.add))
            to_pe(V.tensor_copy(same[:, 0:1], same[:, 0:1]))
            from_pe()
            link(V.tensor_copy(ends[:, :, :].rearrange("a c t -> a (c t)"), psR[0:1, 0:4 * TILES]))
            hk, tk, ft, th = (ends[:, c, :] for c in range(4))
            T = TILES
            lr = link_row
            link(V.memset(lr[:, :, :], 0.0))
            joined, whole, fa, fc, fwd, bwd = (lr[:, c, :] for c in range(6))
            link(V.tensor_tensor(joined[:, 1:T], hk[:, 1:T], tk[:, 0:T - 1], ALU.is_equal))
            link(V.tensor_tensor(whole[:, 0:T], hk, tk, ALU.is_equal))
            link(V.tensor_tensor(fa[:, 1:T], joined[:, 1:T], whole[:, 0:T - 1], ALU.mult))
            link(V.tensor_tensor(fc[:, 1:T], joined[:, 1:T], ft[:, 0:T - 1], ALU.mult))
            link(V.tensor_tensor_scan(fwd[:, 0:T], fa[:, 0:T], fc[:, 0:T], 0.0, ALU.mult, ALU.add))
            link(V.tensor_tensor(fa[:, 0:T - 1], joined[:, 1:T], whole[:, 1:T], ALU.mult))
            link(V.tensor_tensor(fc[:, 0:T - 1], joined[:, 1:T], th[:, 1:T], ALU.mult))
            link(V.memset(fa[:, T - 1:T], 0.0))
            link(V.memset(fc[:, T - 1:T], 0.0))
            link(V.tensor_tensor_scan(bwd[:, 0:T][:, ::-1], fa[:, 0:T][:, ::-1], fc[:, 0:T][:, ::-1], 0.0,
                                      ALU.mult, ALU.add))
            to_pe(V.tensor_copy(ty[:, 1, :], ty[:, 1, :]))
            from_pe()
            link(V.tensor_copy(carryc[:, :], psP[0:TILES, 0:2]))
            for key_col, c in ((0, 0), (P - 1, 1)):
                link(V.tensor_scalar(gate[:, :], keyr[:, :], keyr[:, key_col:key_col + 1], carryc[:, c:c + 1],
                                     ALU.is_equal, ALU.mult))
                link(V.tensor_tensor(runt[:, :], runt[:, :], gate[:, :], ALU.add))
            link(V.tensor_scalar(runt[:, :], runt[:, :], 1.0, None, ALU.max))
            to_pe(V.reciprocal(runf[:, :], runt[:, :]))
            from_pe()
            link(V.tensor_copy(wcol[:, :], psP[:, 0:TILES]))

            from_pe()
            link(V.tensor_copy(need[:, 0, :], psR[0:1, 0:BLOCKS]))
            link(V.tensor_copy(need_i[:, 0, :], need[:, 0, :]))
            link(V.tensor_scalar(need_i[:, 1, :], need_i[:, 0, :], 9, None, ALU.arith_shift_right))
            link(V.tensor_scalar(need[:, 0, :], need[:, 0, :], float(LASTROW), None, ALU.is_ge))
            link(V.tensor_copy(need[:, 1, :], need_i[:, 1, :]))
            link(V.tensor_tensor(need[:, 1, :], need[:, 1, :], need[:, 0, :], ALU.add))
            link(V.tensor_scalar(need[:, 1, :], need[:, 1, :], 1.0, float(STEPS), ALU.add, ALU.min))
            V.tensor_copy(need_i[:, 1, :], need[:, 1, :]).then_inc(s_prep, 1)

            def bn(st, tiles):
                u = st.slot
                for t in tiles:
                    if t == 0:
                        dve.wait_ge(x_in[u], st.use(16, 16))
                    if t == DENSE:
                        dve.wait_ge(g_in[u], st.use(16 * EDGE, 16 * EDGE))
                    tile = xin[u][:, t, :] if t < DENSE else xg[u][:, t - DENSE, :]
                    ins = V.bn_stats(raw[:, t, :], tile)
                return ins

            def aggregate(st):
                n = st.tiles(st.kind)
                for t in range(n):
                    ins = V.bn_aggr(mv[:, t, :], raw[:, t, :])
                ins.then_inc(stats, 1)

            def scales(st):
                u, n = st.slot, st.tiles(st.kind)
                dve.wait_ge(std_ready, st.lin(1, 1))
                V.reciprocal(rstd[u][:, 0:n], std[:, 0:n]).then_inc(inv_ready, 1)
                dve.wait_ge(inv_ready, st.lin(1, 1))
                ins = V.scalar_tensor_tensor(out=nmean[u][:, 0:n], in0=mv[:, 0:n, 0], scalar=-1.0,
                                             in1=rstd[u][:, 0:n], op0=ALU.mult, op1=ALU.mult)
                if st.kind == AGG:
                    ins.then_inc(nm_ready, 1)
                    dve.wait_ge(nm_ready, st.lin(1, 1 - AGG0))
                    V.memset(rstd[u][0:1, DENSE:DENSE + EDGE], 0.0)
                    ins = V.memset(nmean[u][0:1, DENSE:DENSE + EDGE], 0.0)
                ins.then_inc(ln_ready, 1)

            def select(st):
                u = st.slot
                dve.wait_ge(spread, st.lin(1, 1 - AGG0))
                b0 = st.lin(EDGE, -EDGE * AGG0)
                d = cold[:, bass.ds(b0, EDGE)].rearrange("p (k a) -> p k a", a=1).broadcast_to([P, EDGE, P])
                V.tensor_tensor(smat[u][:, :, :], psR[:, 0:EDGE * P].rearrange("p (k e) -> p k e", k=EDGE), d,
                                ALU.is_equal).then_inc(s_ready, 1)

            def finish(st, j):
                pos, pair, edge, v = j
                u = st.slot
                dve.wait_ge(prods, st.job(pos, 1))
                if pair is not None:
                    if pair == 0 and not (st.turn is None and st.base < UNROLL):
                        dve.wait_ge(x_out[u], st.use(16, 0))
                    V.scalar_tensor_tensor(out=xout[u][:, 2 * pair:2 * pair + 2, :], in0=psO[v][:, :, :],
                                           scalar=0.0, in1=xin[u][:, 2 * pair:2 * pair + 2, :],
                                           op0=ALU.max, op1=ALU.add).then_inc(fin, 1)
                elif st.kind == MSG:
                    if edge == 0 and not (st.turn is None and st.base < UNROLL):
                        dve.wait_ge(m_out[u], st.use(16, 0))
                    V.tensor_scalar(mbuf[u][:, edge, :], psO[v][:, 0, :],
                                    wcol[:, bass.ds(st.lin(EDGE, edge), 1)], None, ALU.mult).then_inc(fin, 1)
                else:
                    nxt = st if edge + 1 < EDGE else st.after(1)
                    k = (edge + 1) % EDGE
                    if not (st.turn is None and st.base == ROOT0 - 1 and edge == EDGE - 1):
                        if k == 0:
                            dve.wait_ge(m_in[nxt.slot], nxt.use(16 * EDGE, 16 * EDGE, AGG0))
                        V.tensor_copy(mbuf[nxt.slot][0:1, k, :], psO[v][0:1, 0, :]).then_inc(carry, 1)
                    V.scalar_tensor_tensor(out=orow[:, bass.ds(st.lin(EDGE, edge - EDGE * AGG0), 1), :]
                                           .rearrange("p a f -> p (a f)"), in0=psO[v][:, 0, :],
                                           scalar=0.0, in1=xg[u][:, edge, :],
                                           op0=ALU.max, op1=ALU.add).then_inc(fin, 1)

            def body(st):
                jobs, left = st.jobs(), STEPS if st.turn is not None else STEPS - st.base
                nxt, far = st.after(1), st.after(2)
                if st.turn is None and st.base == AGG0:
                    dve.wait_ge(m_in[st.slot], 16 * EDGE)
                    V.memset(mbuf[st.slot][0:1, 0, :], 0.0).then_inc(carry, 1)
                if left > 1:
                    scales(nxt)
                if st.kind == ROOT:
                    if left > 2:
                        bn(far, range(0, DENSE)).then_inc(bn_raw, 1)
                        dve.wait_ge(bn_raw, far.lin(1, 1))
                    finish(st, jobs[0])
                    if left > 2:
                        aggregate(far)
                    finish(st, jobs[1])
                    return
                finish(st, jobs[0])
                ins = bn(far, range(0, DENSE))
                finish(st, jobs[1])
                if nxt.kind == AGG:
                    select(nxt)
                if far.kind != ROOT:
                    ins = bn(far, range(DENSE, DENSE + EDGE))
                ins.then_inc(bn_raw, 1)
                dve.wait_ge(bn_raw, far.lin(1, 1))
                finish(st, jobs[2])
                aggregate(far)
                finish(st, jobs[3])
                finish(st, jobs[4])

            for s in range(2):
                bn(Step(pl, s), range(0, DENSE + EDGE)).then_inc(bn_raw, 1)
                dve.wait_ge(bn_raw, s + 1)
                aggregate(Step(pl, s))
                if s == 0:
                    scales(Step(pl, 0))
            run_steps(dve, pl, body)

        @block.tensor
        def _(pe):
            MM = nc.tensor.matmul
            ready = [0]

            def from_dve():
                ready[0] += 1
                pe.wait_ge(s_pv, ready[0])

            pe.wait_ge(s_pool, 9)
            from_dve()
            rowtot = total[0:BLOCKS, 0, :]
            MM(psP[0:BLOCKS, 0:R], upper[0:BLOCKS, 0:BLOCKS], rowtot, start=True, stop=True)
            MM(psP[:, 16:16 + R], ones[0:BLOCKS, :], rowtot, start=True, stop=True).then_inc(s_pp, 1)
            from_dve()
            for i, row in enumerate((rowd, rowe, rows, rowk, rowpf[:, 0, :], rowpf[:, 1, :], rowg, rowp, rowo)):
                if i >= 2:
                    from_dve()
                nc.tensor.transpose(turned_rows[i % 2][:, 0:BLOCKS], row[:, 0:P], ident[0:BLOCKS, 0:BLOCKS]).then_inc(s_pp, 1)
            from_dve()
            from_dve()
            def permute(b, i):
                pe.wait_ge(s_lane, b + 1)
                pe.wait_ge(s_tile, b + 1)
                MM(psR[:, 0:2 * TEVEN], lanes[:, i, :], tiles2[:, i, :, :].rearrange("p a q -> p (a q)"),
                   start=(isinstance(b, int) and b == 0),
                   stop=(isinstance(b, int) and b == BLOCKS - 1)).then_inc(s_perm, 1)

            run_blocks(pe, BLOCKS, permute)
            from_dve()
            nc.tensor.transpose(psP[0:TILES, 0:P], keyc[:, :], ident[:, :]).then_inc(s_pp, 1)
            from_dve()
            for c, col in enumerate((keyr[:, 0:1], keyr[:, P - 1:P], runf[:, P - 1:P], runt[:, 0:1])):
                ins = nc.tensor.transpose(psR[0:1, c * TILES:(c + 1) * TILES], col, ident[0:TILES, 0:TILES])
            ins.then_inc(s_pp, 1)
            from_dve()
            for c in range(2):
                ins = MM(psP[0:TILES, c:c + 1], link_row[:, 4 + c, 0:TILES], ones[0:1, 0:1], start=True, stop=True)
            ins.then_inc(s_pp, 1)
            from_dve()
            nc.tensor.transpose(psP[:, 0:TILES], runf[:, :], ident[0:TILES, 0:TILES]).then_inc(s_pp, 1)
            nc.tensor.transpose(psR[0:1, 0:BLOCKS], rowd[:, P - 1:P],
                                ident[0:BLOCKS, 0:BLOCKS]).then_inc(s_pp, 1)
            pe.wait_ge(s_prep, 1)
            pe.wait_ge(s_w, 16 * 2 * KC)

            def turn(st, j):
                pos, pair, edge, v = j
                pe.wait_ge(normed, st.job(pos, 1))
                wait(pe, hT_ready, st.job(pos, 1 - 2))
                for t in range(1 if pair is None else 2):
                    for k in range(KC):
                        ins = nc.tensor.transpose(psT[v % 2][:, t * KC + k, :], h[v][:, t, k * P:(k + 1) * P], ident[:, :])
                ins.then_inc(turned, 1)

            def spread_dst(st):
                if not (st.turn is None and st.base == AGG0):
                    pe.wait_ge(s_ready, st.lin(1, -AGG0))
                pe.wait_ge(e_slot, st.lin(1, 1 - AGG0))
                for k in range(EDGE):
                    e = eslot[st.slot][:, k:k + 1]
                    ins = nc.tensor.transpose(psR[:, k * P:(k + 1) * P], e.broadcast_to([P, P]), ident[:, :])
                ins.then_inc(spread, 1)

            def product(st, j):
                pos, pair, edge, v = j
                if pair is None and st.kind == MSG:
                    r = nc.tensor.value_load(tile_type_i[0:1, bass.ds(st.lin(EDGE, edge), 1)], min_val=0, max_val=R - 1)
                pe.wait_ge(hT_ready, st.job(pos, 1))
                wait(pe, fin, st.job(pos, 1 - SLOTS))
                if pair is not None:
                    MM(psO[v][:, :, :].rearrange("p a f -> p (a f)"), ones3[:, :],
                       bias_rows[:, :, :].rearrange("p a f -> p (a f)"), start=True, stop=False, skip_group_check=True)
                    for t in range(2):
                        for k in range(KC):
                            ins = MM(psO[v][:, t, :], hT[v][:, t * KC + k, :], wr_sb[:, k, :], start=False,
                                     stop=(t == 1 and k == KC - 1), skip_group_check=True)
                elif st.kind == MSG:
                    for k in range(KC):
                        ins = MM(psO[v][:, 0, :], hT[v][:, k, :], w_sb[:, bass.ds(r * F + k * R * F, F)],
                                 start=(k == 0), stop=(k == KC - 1))
                else:
                    u = st.slot
                    MM(psO[v][:, 0, :], ones3_agg[:, :], bias_rows[:, 0, :], start=True, stop=False)
                    for k in range(KC):
                        MM(psO[v][:, 0, :], hT[v][:, k, :], wr_sb[:, k, :], start=False, stop=False)
                    if edge == 0:
                        pe.wait_ge(s_ready, st.lin(1, 1 - AGG0))
                        pe.wait_ge(m_in[u], st.use(16 * EDGE, 16 * EDGE, AGG0))
                    pe.wait_ge(carry, st.lin(EDGE, edge + 1 - EDGE * AGG0))
                    ins = MM(psO[v][:, 0, :], smat[u][:, edge, :], mbuf[u][:, edge, :], start=False, stop=True)
                ins.then_inc(prods, 1)

            def body(st):
                jobs = st.jobs()
                turn(st, jobs[0])
                if not (st.turn is None and st.base == 0):
                    prev = st.after(-1)
                    product(prev, prev.jobs()[-1])
                for a, b in zip(jobs[1:], jobs[:-1]):
                    turn(st, a)
                    product(st, b)
                    if a[0] == 2 and st.next_kind == AGG:
                        spread_dst(st.after(1))

            run_steps(pe, pl, body)
            last = Step(pl, STEPS - 1)
            product(last, last.jobs()[-1])


_INS = ["x", "src", "dst", "edge_type_8", "L0_gnn_W", "L0_gnn_W_root", "L0_gnn_bias"]


def kernel(**inputs):
    import numpy as _np
    import concourse.bacc as _bacc
    from concourse import mybir as _mybir
    from concourse.bass_utils import run_bass_kernel_spmd as _run

    nc = _bacc.Bacc("TRN2", target_bir_lowering=False, num_devices=1)
    arrays, args = {}, []
    for name in _INS:
        a = _np.ascontiguousarray(inputs[name])
        arrays[f"in_{name}_dram"] = a
        args.append(nc.dram_tensor(f"in_{name}_dram", a.shape, _mybir.dt.from_np(a.dtype), kind="ExternalInput").ap())
    out = nc.dram_tensor("out_dram", inputs["x"].shape, _mybir.dt.float32, kind="ExternalOutput").ap()
    build(nc, *args, out)
    r = _run(nc, [arrays], core_ids=[0])
    return r.results[0]["out_dram"]
```

```python
from contextlib import ExitStack

import concourse.bass as bass
from concourse import mybir

F32 = mybir.dt.float32
F32R = mybir.dt.float32r
BF16 = mybir.dt.bfloat16
I32 = mybir.dt.int32
ALU = mybir.AluOpType
ACT = mybir.ActivationFunctionType
AX_X = mybir.AxisListType.X

P = 128
UNROLL = 4
DENSE, PAIRS = 4, 2
SLOTS = 4
EDGE = 3
BIG = 1 << 20
EPS = 1e-05
SORT_BLOCKS = 11
SORT, LINK, MSG, BRIDGE, AGG, ROOT = range(6)
EDGES = (MSG, AGG)
SPLIT = {MSG: (0, 2), BRIDGE: (0, 1), AGG: (0, 2, 4), ROOT: (1,)}


def cdiv(a, b):
    return -(-a // b)


def wait(eng, sem, value):
    if not isinstance(value, int) or value > 0:
        eng.wait_ge(sem, value)


class Plan:

    def __init__(self, n, f, e, r):
        self.N, self.F, self.E, self.R = n, f, e, r
        self.GROUP = P * DENSE
        self.STEPS = cdiv(n, self.GROUP)
        self.BLOCK = P - 1
        self.BLOCKS = cdiv(e, self.BLOCK)
        self.TILES = (e + r * (P - 1)) // P
        assert self.TILES % EDGE == 0 and self.BLOCKS % EDGE == 0 and self.BLOCKS % SORT_BLOCKS == 0
        lengths = [self.BLOCKS // SORT_BLOCKS, 4, self.TILES // EDGE, 1, self.BLOCKS // EDGE]
        lengths.append(self.STEPS - sum(lengths))
        assert min(lengths) > 0
        self.first = [sum(lengths[:k]) for k in range(len(lengths) + 1)]
        self.split0 = [sum(n * self.splits(k) for k, n in enumerate(lengths[:kind])) for kind in range(len(lengths))]
        self.job0 = [sum(n * self.jobs_in(k) for k, n in enumerate(lengths[:kind])) for kind in range(len(lengths))]

    def kind(self, s):
        return max(k for k in (SORT, LINK, MSG, BRIDGE, AGG, ROOT) if self.first[k] <= s)

    def jobs_in(self, kind):
        return EDGE + PAIRS if kind in EDGES else PAIRS

    def splits(self, kind, before=EDGE + PAIRS):
        return sum(pos < before for pos in SPLIT.get(kind, ()))

    def count(self, slot, kinds, before):
        return sum(1 for s in range(before) if s % UNROLL == slot and self.kind(s) in kinds)


class Step:

    def __init__(self, plan, base, turn=None):
        self.plan, self.base, self.turn = plan, base, turn
        self.slot = base % UNROLL
        self.kind = plan.kind(base)
        self.next_kind = plan.kind(base + 1)

    def lin(self, a, c):
        return a * self.base + c if self.turn is None else self.turn * (a * UNROLL) + (a * self.base + c)

    def nth(self, a=1, c=0):
        return self.lin(a, c - a * self.plan.first[self.kind])

    def use(self, scale, c, kinds=range(6)):
        n = self.plan.count(self.slot, kinds, self.base)
        return scale * n + c if self.turn is None else self.turn * scale + (scale * n + c)

    def jobs(self):
        order = [(0, None), (None, 0), (1, None), (None, 1), (None, 2)] if self.kind in EDGES else [(0, None), (1, None)]
        first = Step(self.plan, self.base)
        return [(pos, pair, edge, first.job(pos) % SLOTS) for pos, (pair, edge) in enumerate(order)]

    def job(self, pos, c=0):
        return self.nth(self.plan.jobs_in(self.kind), self.plan.job0[self.kind] + pos + c)

    def last_job(self, c=0):
        return self.job(self.plan.jobs_in(self.kind) - 1, c)

    def is_split(self, pos):
        return pos in SPLIT.get(self.kind, ())

    def nth_split(self, pos, c=0):
        return self.nth(self.plan.splits(self.kind), self.plan.split0[self.kind] + self.plan.splits(self.kind, pos) + c)

    def scaled_early(self):
        return self.base > 0 and self.plan.kind(self.base - 1) == MSG

    def back(self, pos, k):
        st = self
        while pos < k:
            if st.turn is None and st.base == 0:
                return None
            st, pos = st.after(-1), pos + len(st.after(-1).jobs())
        return st, pos - k

    def tiles(self):
        return DENSE + EDGE if self.kind in EDGES else DENSE

    def after(self, k):
        return Step(self.plan, self.base + k, self.turn)


def run_steps(eng, plan, body, ends=None):
    for a, b in zip(plan.first[:-1], plan.first[1:]):
        if b <= (ends or plan.STEPS):
            head = a + UNROLL
            turns = (min(b, plan.STEPS - 1) - UNROLL - head) // UNROLL
            if turns < 2:
                head, turns = b, 0
            for s in range(a, head):
                body(Step(plan, s))
            if turns:
                with eng.Fori(0, turns) as turn:
                    for c in range(UNROLL):
                        body(Step(plan, head + c, turn))
            for s in range(head + UNROLL * turns, b):
                body(Step(plan, s))


def build(nc, x, src, dst, etype, W, W_root, bias, out):
    N, F = x.shape
    R = W.shape[0]
    E = src.shape[0]
    KC = F // P
    pl = Plan(N, F, E, R)
    BLOCK, BLOCKS, TILES, STEPS = pl.BLOCK, pl.BLOCKS, pl.TILES, pl.STEPS
    MSG0, AGG0, ROOT0 = (pl.first[k] for k in (MSG, AGG, ROOT))
    SORT_RING = 2 * SORT_BLOCKS
    COLS = TILES + BLOCKS
    TEVEN = TILES + TILES % 2
    LASTROW = N - pl.GROUP
    PAD = N + 10000
    assert F == 2 * P and PAD + 1 < (1 << 16) and TILES <= P and BLOCKS <= P

    ctx = ExitStack()
    with ctx:
        def sb(name, shape, dt=F32):
            return ctx.enter_context(nc.sbuf_tensor(name, shape, dt))

        early = ExitStack()

        def pre(name, shape, dt=F32):
            return early.enter_context(nc.sbuf_tensor(name, shape, dt))

        def ps(name, shape, dt=F32):
            return ctx.enter_context(nc.psum_tensor(name, shape, dt))

        def sem(name):
            return ctx.enter_context(nc.semaphore(name))

        msgs = nc.dram_tensor("msgs", [TILES * P, F], F32, kind="Internal").ap()

        w_sb = sb("w_sb", [P, KC * R * F])
        wr_sb = sb("wr_sb", [P, KC, F])
        wr_a = sb("wr_a", [P, KC, F], F32R)
        wr_b = sb("wr_b", [P, KC, F], F32R)
        ident = sb("ident", [P, P])
        eps = sb("eps", [P, 1])
        bias_rows = sb("bias_rows", [P, 2, F], BF16)
        ones3 = sb("ones3", [P, P], BF16)
        ones3_agg = sb("ones3_agg", [P, P], BF16)
        cold = sb("cold", [P, BLOCKS])
        cole = sb("cole", [P, BLOCKS])
        gidx = sb("gidx", [P, COLS], I32)
        midx = sb("midx", [P, BLOCKS], I32)
        oidx = sb("oidx", [P, BLOCKS], I32)
        wcol = sb("wcol", [P, TILES])
        tile_type_i = sb("tile_type_i", [1, TILES], I32)
        need_i = sb("need_i", [1, 2, BLOCKS], I32)
        xin = [sb(f"xin{u}", [P, DENSE, F]) for u in range(UNROLL)]
        xout = [sb(f"xout{u}", [P, DENSE, F]) for u in range(2)]
        xg = [sb(f"xg{u}", [P, EDGE, F]) for u in range(UNROLL)]
        mbuf = [sb(f"mbuf{u}", [P, EDGE, F]) for u in range(UNROLL)]
        smat = [sb(f"smat{u}", [P, EDGE, P]) for u in range(2)]
        gslot = [sb(f"gslot{u}", [P, EDGE], I32) for u in range(UNROLL)]
        mslot = [sb(f"mslot{u}", [P, EDGE], I32) for u in range(UNROLL)]
        eslot = [sb(f"eslot{u}", [P, EDGE]) for u in range(UNROLL)]
        raw = [sb(f"raw{u}", [P, DENSE + EDGE, 6]) for u in range(2)]
        mv = [sb(f"mv{u}", [P, DENSE + EDGE, 2]) for u in range(2)]
        std = [sb(f"std{u}", [P, DENSE + EDGE]) for u in range(2)]
        rstd = [sb(f"rstd{u}", [P, DENSE + EDGE]) for u in range(UNROLL)]
        nmean = [sb(f"nmean{u}", [P, DENSE + EDGE]) for u in range(UNROLL)]
        h = [sb(f"h{v}", [P, 2, F]) for v in range(SLOTS)]
        hT = [sb(f"hT{v}", [P, 2 * KC, P]) for v in range(SLOTS)]
        hT_a = [sb(f"hT_a{v}", [P, 2 * KC, P], F32R) for v in range(SLOTS)]
        hT_b = [sb(f"hT_b{v}", [P, 2 * KC, P], F32R) for v in range(2)]
        upper = pre("upper", [P, P])
        ones = pre("ones", [P, P])
        iota_i = pre("iota_i", [P, P], I32)
        iota_f = pre("iota_f", [P, P])
        bias3 = pre("bias3", [3, F])
        bpart = pre("bpart", [3, 3, F], BF16)
        bres = pre("bres", [3, F])
        bown = pre("bown", [3, 3, F])
        rowd_i = pre("rowd_i", [BLOCKS, P + 1], I32)
        rows_i = pre("rows_i", [BLOCKS, P], I32)
        rowt_i = pre("rowt_i", [BLOCKS, P], I32)
        rowd = pre("rowd", [BLOCKS, P + 1])
        rows = pre("rows", [BLOCKS, P])
        rowt = pre("rowt", [BLOCKS, P])
        rowe = pre("rowe", [BLOCKS, P])
        rowx = pre("rowx", [BLOCKS, P])
        rowo = pre("rowo", [BLOCKS, P])
        rowg = pre("rowg", [BLOCKS, P])
        rowk = pre("rowk", [BLOCKS, P])
        onehot = pre("onehot", [BLOCKS, R, BLOCK])
        notfirst = pre("notfirst", [BLOCKS, R, BLOCK])
        rank = pre("rank", [BLOCKS, R, BLOCK])
        types_i = pre("types_i", [P, R], I32)
        types = pre("types", [P, R])
        total = pre("total", [P, 8, R])
        total_i = pre("total_i", [P, 2, R], I32)
        rowp = pre("rowp", [BLOCKS, P])
        rowp_i = pre("rowp_i", [BLOCKS, 3, P], I32)
        rowpf = pre("rowpf", [BLOCKS, 2, P])
        cols_ = pre("cols_", [P, BLOCKS])
        colk = pre("colk", [P, BLOCKS])
        coll = pre("coll", [P, BLOCKS])
        colq = pre("colq", [P, BLOCKS])
        lanes = pre("lanes", [P, SORT_RING, P])
        tiles2 = pre("tiles2", [P, SORT_RING, 2, TEVEN])
        keyc = pre("keyc", [P, TILES])
        keyr = pre("keyr", [TILES, P])
        same = pre("same", [TILES, P + 1])
        runf = pre("runf", [TILES, P])
        runt = pre("runt", [TILES, P])
        gate = pre("gate", [TILES, P])
        ends = pre("ends", [1, 4, TILES])
        link_row = pre("link_row", [1, 6, TILES + 1])
        carryc = pre("carryc", [TILES, 2])
        begun = pre("begun", [1, R - 1, TILES])
        tile_type = pre("tile_type", [1, TILES])
        need = pre("need", [1, 2, BLOCKS])
        early.close()
        orow = sb("orow", [P, BLOCKS, F])

        psT = [ps(f"psT{v}", [P, 2 * KC, P]) for v in range(2)]
        psO = [ps(f"psO{v}", [P, 2, F]) for v in range(SLOTS)]
        psR = ps("psR", [P, 512])
        psP = ps("psP", [P, 512])
        turned_rows = (psP, psR)

        s_wr = sem("s_wr")
        s_w = sem("s_w")
        s_brows = sem("s_brows")
        rows_made = sem("rows_made")
        s_bias = sem("s_bias")
        s_list = sem("s_list")
        s_fill = sem("s_fill")
        s_pool = sem("s_pool")
        s_c = sem("s_c")
        s_pp = sem("s_pp")
        s_pv = sem("s_pv")
        s_lane = sem("s_lane")
        s_tile = sem("s_tile")
        s_perm = sem("s_perm")
        s_gidx = sem("s_gidx")
        s_types = sem("s_types")
        s_need = sem("s_need")
        s_eps = sem("s_eps")
        x_in = [sem(f"x_in{u}") for u in range(UNROLL)]
        x_out = [sem(f"x_out{u}") for u in range(UNROLL)]
        g_in = [sem(f"g_in{u}") for u in range(UNROLL)]
        m_in = [sem(f"m_in{u}") for u in range(UNROLL)]
        m_out = [sem(f"m_out{u}") for u in range(UNROLL)]
        idx_ready = sem("idx_ready")
        fetches = sem("fetches")
        e_slot = sem("e_slot")
        bn_raw = sem("bn_raw")
        stats = sem("stats")
        std_ready = sem("std_ready")
        inv_ready = sem("inv_ready")
        nm_ready = sem("nm_ready")
        ln_ready = sem("ln_ready")
        normed = sem("normed")
        turned = sem("turned")
        hT_ready = sem("hT_ready")
        hb_ready = sem("hb_ready")
        wa_ready = sem("wa_ready")
        wb_ready = sem("wb_ready")
        prods = sem("prods")
        fin = sem("fin")
        spread = sem("spread")
        s_ready = sem("s_ready")
        carry = sem("carry")
        rows_out = sem("rows_out")
        s_scat = sem("s_scat")

        block = ctx.enter_context(nc.Block())

        def node_rows(t, st):
            if st.turn is None:
                r0 = min(st.base * pl.GROUP, LASTROW)
                v = t[r0:r0 + pl.GROUP, :]
            else:
                v = t[bass.ds(st.lin(pl.GROUP, 0), pl.GROUP), :]
            return v.rearrange("(p j) f -> p (j f)", p=P)

        def flat(t):
            return t[:, :, :].rearrange("p a b -> p (a b)")

        @block.sync
        def _(sp):
            LAST = BLOCKS - 1
            TAIL = E - (BLOCK * LAST - 1)
            sp.wait_ge(s_fill, 3)
            n_list = 0
            for row, lst, width in ((rowd_i, dst, P + 1), (rows_i, src, P), (rowt_i, etype, P)):
                body = bass.AP(tensor=lst.tensor, offset=BLOCK - 1, ap=[[BLOCK, LAST - 1], [1, width]])
                sp.dma_start(row[1:LAST, 0:width], body).then_inc(s_list, 16)
                sp.dma_start(row[0:1, 1:width],
                             lst[0:width - 1].rearrange("(a c) -> a c", a=1)).then_inc(s_list, 16)
                sp.dma_start(row[LAST:LAST + 1, 0:TAIL],
                             lst[E - TAIL:E].rearrange("(a c) -> a c", a=1)).then_inc(s_list, 16)
            b1 = bias.rearrange("(a c) -> a c", a=1)
            for j in range(3):
                sp.dma_start(bias3[j:j + 1, :], b1).then_inc(s_bias, 16)
            for u in range(2):
                sp.dma_start(flat(xin[u]), node_rows(x, Step(pl, u))).then_inc(x_in[u], 16)
            for k in range(KC):
                sp.dma_start(wr_sb[:, k, :], W_root[k * P:(k + 1) * P, :]).then_inc(s_wr, 16)
            for u in range(2, UNROLL):
                sp.dma_start(flat(xin[u]), node_rows(x, Step(pl, u))).then_inc(x_in[u], 16)
            for k in range(KC):
                sp.dma_start(w_sb[:, k * R * F:(k + 1) * R * F].rearrange("p (r o) -> p r o", r=R),
                             W[:, k * P:(k + 1) * P, :].rearrange("r p o -> p r o")).then_inc(s_w, 16)

            def relay(st):
                sp.wait_ge(x_out[st.slot], st.use(16, 16))
                sp.sem_inc(rows_out, 1)

            def body(st):
                u = st.slot
                pos = 2 if st.kind in EDGES else 1
                sp.wait_ge(fin, st.job(pos, 1))
                last = st.turn is None and st.base == STEPS - 1
                if last:
                    relay(st.after(-1))
                sp.dma_start(node_rows(out, st), flat(xout[u % 2])).then_inc(x_out[u], 16)
                if st.turn is not None or st.base + UNROLL < STEPS:
                    sp.dma_start(flat(xin[u]), node_rows(x, st.after(UNROLL))).then_inc(x_in[u], 16)
                if st.kind == MSG:
                    sp.wait_ge(fin, st.job(4, 1))
                    sp.dma_start(msgs[bass.ds(st.nth(EDGE * P), EDGE * P), :].rearrange("(k p) f -> p k f", k=EDGE),
                                 mbuf[u][:, :, :]).then_inc(m_out[u], 16)
                if not last and not (st.turn is None and st.base == 0):
                    relay(st.after(-1))

            run_steps(sp, pl, body)
            relay(Step(pl, STEPS - 1))

        @block.gpsimd
        def _(pool):
            nc.gpsimd.memset(rowd_i[:, :], PAD).then_inc(s_fill, 1)
            nc.gpsimd.memset(rows_i[:, :], 0).then_inc(s_fill, 1)
            nc.gpsimd.memset(rowt_i[:, :], R).then_inc(s_fill, 1)
            nc.gpsimd.iota(iota_i[:, :], [[1, P]], base=0, channel_multiplier=0).then_inc(s_pool, 1)
            nc.gpsimd.iota(types_i[:, :], [[1, R]], base=0, channel_multiplier=0).then_inc(s_pool, 1)
            nc.gpsimd.memset(ident[:, :], 0.0).then_inc(s_pool, 1)
            nc.gpsimd.memset(upper[:, :], 0.0).then_inc(s_pool, 1)
            nc.gpsimd.memset(ones[:, :], 1.0).then_inc(s_pool, 1)
            nc.gpsimd.memset(notfirst[:, :, :], 1.0).then_inc(s_pool, 1)
            nc.gpsimd.memset(eps[:, :], EPS).then_inc(s_eps, 1)
            pool.wait_ge(s_pool, 6)
            nc.gpsimd.affine_select(out=ident[:, :], in_=ident[:, :], compare_op=ALU.not_equal, fill=1.0,
                                    base=0, pattern=[[-1, P]], channel_multiplier=1).then_inc(s_pool, 1)
            nc.gpsimd.affine_select(out=upper[:, :], in_=upper[:, :], compare_op=ALU.is_ge, fill=1.0,
                                    base=0, pattern=[[-1, P]], channel_multiplier=1).then_inc(s_pool, 1)
            nc.gpsimd.memset(notfirst[:, :, 0:1], 0.0).then_inc(s_pool, 1)
            chain = [0]

            def link(ins):
                chain[0] += 1
                ins.then_inc(s_brows, 1)
                pool.wait_ge(s_brows, chain[0])

            G = nc.gpsimd
            pool.wait_ge(s_pool, 9)
            pool.wait_ge(s_bias, 48)
            link(G.memset(bias_rows[:, :, :], 0.0))
            for k in range(3):
                link(G.tensor_copy(bpart[:, k, :], bias3[:, :] if k == 0 else bres[:, :]))
                if k < 2:
                    link(G.tensor_tensor(bres[:, :], bias3[:, :] if k == 0 else bres[:, :], bpart[:, k, :], ALU.subtract))
            for k in range(3):
                link(G.tensor_scalar(bown[:, k, :], bpart[:, k, :], ident[0:3, k:k + 1], None, ALU.mult))
            for k in (1, 2):
                link(G.tensor_tensor(bown[:, 0, :], bown[:, 0, :], bown[:, k, :], ALU.add))
            for t in range(2):
                link(G.tensor_copy(bias_rows[0:3, t, :], bown[:, 0, :]))
            link(G.memset(ones3[:, :], 0.0))
            link(G.memset(ones3[0:3, :], 1.0))
            link(G.tensor_copy(ones3_agg[:, :], ones3[:, :]))
            link(G.memset(ones3_agg[:, 0:1], 0.0))
            pool.sem_inc(rows_made, 1)
            pool.wait_ge(s_pv, 7)
            for b in range(BLOCKS):
                wait(pool, s_perm, b - SORT_RING + 1)
                nc.gpsimd.tensor_scalar(lanes[:, b % SORT_RING, :], iota_f[:, :], coll[:, b:b + 1], None,
                                        ALU.is_equal).then_inc(s_lane, 1)

            def slot_indices(slot, cols):
                nc.gpsimd.tensor_copy(slot[:, :], cols).then_inc(idx_ready, 1)

            def gather_x(st):
                u = st.slot
                for k in range(EDGE):
                    nc.gpsimd.indirect_dma_start(
                        out=xg[u][:, k, :], out_offset=None, in_=x[:, :],
                        in_offset=bass.IndirectOffsetOnAxis(ap=gslot[u][:, k:k + 1], axis=0)).then_inc(g_in[u], 16)

            def gather_m(st):
                u = st.slot
                for k in range(EDGE):
                    nc.gpsimd.indirect_dma_start(
                        out=mbuf[u][:, k, :], out_offset=None, in_=msgs[:, :],
                        in_offset=bass.IndirectOffsetOnAxis(ap=mslot[u][:, k:k + 1], axis=0)).then_inc(m_in[u], 16)

            order = [("x", s) for s in range(MSG0, MSG0 + UNROLL)]
            for s in range(MSG0, ROOT0):
                if pl.kind(s + UNROLL) in EDGES:
                    order.append(("x", s + UNROLL))
                if s + 1 == pl.first[MSG + 1]:
                    order += [("m", t) for t in range(AGG0, AGG0 + UNROLL)]
                if s >= AGG0 and s + UNROLL < ROOT0:
                    order.append(("m", s + UNROLL))

            def copies(rows, st):
                n = order.index((rows, st.base)) + 1
                return n if st.turn is None else st.turn * (UNROLL * (2 if st.kind == AGG else 1)) + n

            def edge_cols(st):
                return bass.ds(st.nth(EDGE, 0 if st.kind == MSG else TILES), EDGE)

            def fetch_x(st):
                slot_indices(gslot[st.slot], gidx[:, edge_cols(st)])
                if st.kind == AGG:
                    nc.gpsimd.tensor_copy(eslot[st.slot][:, :], cole[:, bass.ds(st.nth(EDGE), EDGE)]).then_inc(e_slot, 1)
                pool.wait_ge(idx_ready, copies("x", st))
                pool.sem_inc(fetches, 1)
                gather_x(st)

            def fetch_m(st):
                slot_indices(mslot[st.slot], midx[:, bass.ds(st.nth(EDGE), EDGE)])
                pool.wait_ge(idx_ready, copies("m", st))
                pool.sem_inc(fetches, 1)
                gather_m(st)

            pool.wait_ge(s_gidx, 1)
            for s in range(MSG0, MSG0 + UNROLL):
                fetch_x(Step(pl, s))

            def body(st):
                nxt = st.after(UNROLL)
                if st.kind < MSG:
                    return
                if nxt.kind in EDGES:
                    pool.wait_ge(fin, st.last_job(1))
                    fetch_x(nxt)
                if st.turn is None and st.base + 1 == pl.first[MSG + 1]:
                    for u in range(UNROLL):
                        pool.wait_ge(m_out[u], 16 * pl.count(u, (MSG,), STEPS))
                    for s in range(AGG0, AGG0 + UNROLL):
                        fetch_m(Step(pl, s))
                if st.kind == AGG and nxt.kind == AGG:
                    fetch_m(nxt)

            run_steps(pool, pl, body, ends=ROOT0)
            pool.wait_ge(s_need, 1)
            for b in range(BLOCKS):
                if b % EDGE == 0:
                    pool.wait_ge(fin, Step(pl, AGG0 + b // EDGE).last_job(1))
                steps_needed = nc.gpsimd.value_load(need_i[0:1, 1, b:b + 1], min_val=1, max_val=STEPS)
                pool.wait_ge(rows_out, steps_needed)
                pool.sem_inc(fetches, 1)
                nc.gpsimd.indirect_dma_start(
                    out=out[:, :], out_offset=bass.IndirectOffsetOnAxis(ap=oidx[:, b:b + 1], axis=0),
                    in_=orow[:, b, :], in_offset=None, bounds_check=N - 1, oob_is_err=False).then_inc(s_scat, 16)
            pool.wait_ge(s_scat, 16 * BLOCKS)

        @block.scalar
        def _(act):
            act.wait_ge(s_eps, 1)

            def deviations(st):
                n = st.tiles()
                act.wait_ge(stats, st.lin(1, 1))
                nc.scalar.activation(std[st.slot % 2][:, 0:n], mv[st.slot % 2][:, 0:n, 1], ACT.Sqrt, bias=eps[:, 0:1]).then_inc(std_ready, 1)

            def norm(st, j):
                pos, pair, edge, v = j
                u = st.slot
                if pos == 0:
                    act.wait_ge(ln_ready, st.lin(1, 1))
                wait(act, turned, st.job(pos, 1 - SLOTS))
                if pair is None:
                    t = DENSE + edge
                    ins = nc.scalar.activation(h[v][:, 0, :], xg[u][:, edge, :], ACT.Relu,
                                               scale=rstd[u][:, t:t + 1], bias=nmean[u][:, t:t + 1])
                else:
                    for c in range(2):
                        t = 2 * pair + c
                        ins = nc.scalar.activation(h[v][:, c, :], xin[u][:, t, :], ACT.Relu,
                                                   scale=rstd[u][:, t:t + 1], bias=nmean[u][:, t:t + 1])
                ins.then_inc(normed, 1)

            def evacuate(st, j):
                pos, pair, edge, v = j
                act.wait_ge(turned, st.job(pos, 1))
                wait(act, prods, st.job(pos, 1 - SLOTS))
                n = KC if pair is None else 2 * KC
                into = hT_a if st.is_split(pos) else hT
                nc.scalar.activation(into[v][:, 0:n, :], psT[v % 2][:, 0:n, :], ACT.Copy).then_inc(hT_ready, 1)

            def carry_on(st, j):
                pos, pair, edge, v = j
                if st.kind != AGG or pair is not None or (st.turn is None and st.base == ROOT0 - 1 and edge == EDGE - 1):
                    return
                nxt = st if edge + 1 < EDGE else st.after(1)
                k = (edge + 1) % EDGE
                if k == 0:
                    act.wait_ge(m_in[nxt.slot], nxt.use(16 * EDGE, 16 * EDGE, (AGG,)))
                act.wait_ge(prods, st.job(pos, 1))
                nc.scalar.activation(mbuf[nxt.slot][0:1, k, :], psO[v][0:1, 0, :], ACT.Copy).then_inc(carry, 1)

            def body(st):
                jobs, left = st.jobs(), STEPS if st.turn is not None else STEPS - st.base
                if st.scaled_early() and st.kind != MSG:
                    deviations(st.after(1))
                for i, j in enumerate(jobs):
                    evacuate(st, j)
                    if i + 2 < len(jobs):
                        norm(st, jobs[i + 2])
                    elif left > 1:
                        nxt = st.after(1)
                        norm(nxt, nxt.jobs()[i + 2 - len(jobs)])
                    if i:
                        carry_on(st, jobs[i - 1])
                    elif not (st.turn is None and st.base == 0):
                        carry_on(st.after(-1), st.after(-1).jobs()[-1])
                    if i == 0 and st.scaled_early() and st.kind == MSG:
                        deviations(st.after(1))
                if left > 2 and st.kind != MSG:
                    deviations(st.after(2))

            for s in range(2):
                deviations(Step(pl, s))
            for j in Step(pl, 0).jobs()[:2]:
                norm(Step(pl, 0), j)
            act.wait_ge(s_wr, 16 * KC)
            nc.scalar.activation(wr_a[:, :, :], wr_sb[:, :, :], ACT.Copy).then_inc(wa_ready, 1)
            run_steps(act, pl, body)

        @block.vector
        def _(dve):
            chain = [0]

            def link(ins):
                chain[0] += 1
                ins.then_inc(s_c, 1)
                dve.wait_ge(s_c, chain[0])

            V = nc.vector
            pe_done = [0]

            def from_pe():
                pe_done[0] += 1
                dve.wait_ge(s_pp, pe_done[0])

            def to_pe(ins):
                ins.then_inc(s_pv, 1)

            def bn(st, tiles):
                u = st.slot
                for t in tiles:
                    if t == 0:
                        dve.wait_ge(x_in[u], st.use(16, 16))
                    if t == DENSE:
                        dve.wait_ge(g_in[u], st.use(16 * EDGE, 16 * EDGE, EDGES))
                    tile = xin[u][:, t, :] if t < DENSE else xg[u][:, t - DENSE, :]
                    ins = V.bn_stats(raw[st.slot % 2][:, t, :], tile)
                return ins

            def aggregate(st):
                n = st.tiles()
                for t in range(n):
                    ins = V.bn_aggr(mv[st.slot % 2][:, t, :], raw[st.slot % 2][:, t, :])
                ins.then_inc(stats, 1)

            def scales(st):
                u, n = st.slot, st.tiles()
                dve.wait_ge(std_ready, st.lin(1, 1))
                V.reciprocal(rstd[u][:, 0:n], std[u % 2][:, 0:n]).then_inc(inv_ready, 1)
                dve.wait_ge(inv_ready, st.lin(1, 1))
                ins = V.scalar_tensor_tensor(out=nmean[u][:, 0:n], in0=mv[u % 2][:, 0:n, 0], scalar=-1.0,
                                             in1=rstd[u][:, 0:n], op0=ALU.mult, op1=ALU.mult)
                if st.kind == AGG:
                    ins.then_inc(nm_ready, 1)
                    dve.wait_ge(nm_ready, st.nth(1, 1))
                    V.memset(rstd[u][0:1, DENSE:DENSE + EDGE], 0.0)
                    ins = V.memset(nmean[u][0:1, DENSE:DENSE + EDGE], 0.0)
                ins.then_inc(ln_ready, 1)

            def statistics(s):
                bn(Step(pl, s), range(DENSE)).then_inc(bn_raw, 1)
                dve.wait_ge(bn_raw, s + 1)
                aggregate(Step(pl, s))

            dve.wait_ge(s_pool, 9)
            link(V.tensor_copy(iota_f[:, :], iota_i[:, :]))
            link(V.tensor_copy(types[:, :], types_i[:, :]))
            dve.wait_ge(s_list, 16 * 9)
            link(V.tensor_copy(rowd[:, :], rowd_i[:, :]))
            link(V.tensor_copy(rows[:, :], rows_i[:, :]))
            link(V.tensor_copy(rowt[:, :], rowt_i[:, :]))
            link(V.tensor_copy(rowe[:, :], rowd[:, 0:P]))
            link(V.tensor_copy(rowe[:, 0:1], rowd[:, P - 1:P]))
            link(V.tensor_tensor(rowx[:, :], rowd[:, 0:P], rowd[:, 1:P + 1], ALU.is_equal))
            link(V.scalar_tensor_tensor(out=rowo[:, :], in0=rowx[:, :], scalar=float(BIG), in1=rowd[:, 0:P],
                                        op0=ALU.mult, op1=ALU.add))
            link(V.memset(rowo[:, 0:1], float(BIG)))
            link(V.tensor_scalar(rowg[:, :], rowd[:, 0:P], float(N - 1), None, ALU.min))
            link(V.scalar_tensor_tensor(out=rowk[:, :], in0=rowt[:, :], scalar=65536.0, in1=rowd[:, 0:P],
                                        op0=ALU.mult, op1=ALU.add))
            link(V.tensor_scalar(rowk[:, :], rowk[:, :], 1.0, None, ALU.add))

            tb = rowt[:, 1:P].rearrange("b (a j) -> b a j", a=1).broadcast_to([BLOCKS, R, BLOCK])
            yb = types[0:BLOCKS, :].rearrange("b (r a) -> b r a", a=1).broadcast_to([BLOCKS, R, BLOCK])
            link(V.tensor_tensor(onehot[:, :, :], tb, yb, ALU.is_equal))
            link(V.tensor_tensor_scan(flat(rank), flat(notfirst), flat(onehot), 0.0, ALU.mult, ALU.add))
            rowtot = total[0:BLOCKS, 0, :]
            to_pe(V.tensor_copy(rowtot, rank[:, :, BLOCK - 1]))
            statistics(0)
            statistics(1)
            from_pe()
            link(V.tensor_scalar(total[:, 1, :], psP[:, 16:16 + R], float(P - 1), None, ALU.add))
            link(V.tensor_copy(total_i[:, 0, :], total[:, 1, :]))
            link(V.tensor_scalar(total_i[:, 1, :], total_i[:, 0, :], 7, None, ALU.arith_shift_right))
            link(V.tensor_copy(total[:, 2, :], total_i[:, 1, :]))
            link(V.tensor_tensor_scan(total[:, 3, :], ones[:, 0:R], total[:, 2, :], 0.0, ALU.mult, ALU.add))
            link(V.tensor_tensor(total[:, 4, :], total[:, 3, :], total[:, 2, :], ALU.subtract))
            link(V.scalar_tensor_tensor(out=total[0:BLOCKS, 5, :], in0=total[0:BLOCKS, 4, :], scalar=float(P),
                                        in1=psP[0:BLOCKS, 0:R], op0=ALU.mult, op1=ALU.add))
            link(V.tensor_scalar(total[0:BLOCKS, 5, :], total[0:BLOCKS, 5, :], -1.0, None, ALU.add))
            ob = total[0:BLOCKS, 5, :].rearrange("b (r a) -> b r a", a=1).broadcast_to([BLOCKS, R, BLOCK])
            for s in range(2):
                scales(Step(pl, s))
            link(V.tensor_tensor(rank[:, :, :], rank[:, :, :], ob, ALU.add))
            link(V.tensor_tensor(rank[:, :, :], rank[:, :, :], onehot[:, :, :], ALU.mult))
            link(V.memset(rowp[:, 0:1], 0.0))
            link(V.tensor_reduce(rowp[:, 1:P], rank[:, :, :].rearrange("b r j -> b j r"), AX_X, ALU.add))
            link(V.tensor_copy(rowp_i[:, 0, :], rowp[:, :]))
            link(V.tensor_scalar(rowp_i[:, 1, :], rowp_i[:, 0, :], P - 1, None, ALU.bitwise_and))
            link(V.tensor_scalar(rowp_i[:, 2, :], rowp_i[:, 0, :], 7, None, ALU.arith_shift_right))
            link(V.tensor_copy(rowpf[:, 0, :], rowp_i[:, 1, :]))
            link(V.tensor_copy(rowpf[:, 1, :], rowp_i[:, 2, :]))
            link(V.tensor_scalar(rowx[:, :], rowt[:, :], float(R), float(BIG), ALU.is_ge, ALU.mult))
            link(V.tensor_tensor(rowpf[:, 1, :], rowpf[:, 1, :], rowx[:, :], ALU.add))
            link(V.memset(rowpf[:, 1, 0:1], float(BIG)))

            for i, (row, col) in enumerate(((rowd, cold), (rowe, cole), (rows, cols_), (rowk, colk),
                                            (rowpf[:, 0, :], coll), (rowpf[:, 1, :], colq),
                                            (rowg, gidx[:, TILES:COLS]), (rowp, midx), (rowo, oidx))):
                if i == 0:
                    to_pe(V.tensor_copy(rank[0:1, 0, 0:1], rowd[0:1, 0:1]))
                from_pe()
                V.tensor_copy(col if i == 6 else col[:, :], turned_rows[i % 2][:, 0:BLOCKS]).then_inc(s_pv, 1)

            def one_hot_tiles(b):
                wait(dve, s_perm, b - SORT_RING + 1)
                for c, val in enumerate((cols_, colk)):
                    ins = V.tensor_scalar(tiles2[:, b % SORT_RING, c, :], iota_f[:, 0:TEVEN], colq[:, b:b + 1],
                                          val[:, b:b + 1], ALU.is_equal, ALU.mult)
                ins.then_inc(s_tile, 1)

            def take_keys():
                dve.wait_ge(s_perm, BLOCKS)
                V.tensor_copy(gidx[:, 0:TILES], psR[:, 0:TILES]).then_inc(s_gidx, 1)
                to_pe(V.tensor_copy(keyc[:, :], psR[:, TEVEN:TEVEN + TILES]))

                qb = iota_f[0:1, 0:TILES].rearrange("a (r q) -> a r q", r=1).broadcast_to([1, R - 1, TILES])
                eb = total[0:1, 3, 0:R - 1].rearrange("a (r q) -> a r q", q=1).broadcast_to([1, R - 1, TILES])
                link(V.tensor_tensor(begun[:, :, :], qb, eb, ALU.is_ge))
                link(V.tensor_reduce(tile_type[:, :], begun[:, :, :].rearrange("a r q -> a q r"), AX_X, ALU.add))
                V.tensor_copy(tile_type_i[:, :], tile_type[:, :]).then_inc(s_types, 1)

            def run_lengths():
                from_pe()
                link(V.tensor_copy(keyr[:, :], psP[0:TILES, 0:P]))
                link(V.memset(same[:, :], 0.0))
                link(V.tensor_tensor(same[:, 1:P], keyr[:, 1:P], keyr[:, 0:P - 1], ALU.is_equal))
                link(V.tensor_tensor_scan(runf[:, :], same[:, 0:P], ones[0:TILES, :], 0.0, ALU.mult, ALU.add))
                link(V.tensor_scalar(gate[:, :], same[:, 1:P + 1], -1.0, 1.0, ALU.mult, ALU.add))
                link(V.tensor_tensor(gate[:, :], gate[:, :], runf[:, :], ALU.mult))
                link(V.tensor_tensor_scan(runt[:, ::-1], same[:, P:0:-1], gate[:, ::-1], 0.0, ALU.mult, ALU.add))
                to_pe(V.tensor_copy(same[:, 0:1], same[:, 0:1]))

            def join_runs():
                from_pe()
                link(V.tensor_copy(ends[:, :, :].rearrange("a c t -> a (c t)"), psR[0:1, 0:4 * TILES]))
                hk, tk, ft, th = (ends[:, c, :] for c in range(4))
                T = TILES
                lr = link_row
                link(V.memset(lr[:, :, :], 0.0))
                joined, whole, fa, fc, fwd, bwd = (lr[:, c, :] for c in range(6))
                link(V.tensor_tensor(joined[:, 1:T], hk[:, 1:T], tk[:, 0:T - 1], ALU.is_equal))
                link(V.tensor_tensor(whole[:, 0:T], hk, tk, ALU.is_equal))
                link(V.tensor_tensor(fa[:, 1:T], joined[:, 1:T], whole[:, 0:T - 1], ALU.mult))
                link(V.tensor_tensor(fc[:, 1:T], joined[:, 1:T], ft[:, 0:T - 1], ALU.mult))
                link(V.tensor_tensor_scan(fwd[:, 0:T], fa[:, 0:T], fc[:, 0:T], 0.0, ALU.mult, ALU.add))
                link(V.tensor_tensor(fa[:, 0:T - 1], joined[:, 1:T], whole[:, 1:T], ALU.mult))
                link(V.tensor_tensor(fc[:, 0:T - 1], joined[:, 1:T], th[:, 1:T], ALU.mult))
                link(V.memset(fa[:, T - 1:T], 0.0))
                link(V.memset(fc[:, T - 1:T], 0.0))
                link(V.tensor_tensor_scan(bwd[:, 0:T][:, ::-1], fa[:, 0:T][:, ::-1], fc[:, 0:T][:, ::-1], 0.0,
                                          ALU.mult, ALU.add))
                to_pe(V.tensor_copy(tile_type[:, :], tile_type[:, :]))

            def run_weights():
                from_pe()
                link(V.tensor_copy(carryc[:, :], psP[0:TILES, 0:2]))
                for key_col, c in ((0, 0), (P - 1, 1)):
                    link(V.tensor_scalar(gate[:, :], keyr[:, :], keyr[:, key_col:key_col + 1], carryc[:, c:c + 1],
                                         ALU.is_equal, ALU.mult))
                    link(V.tensor_tensor(runt[:, :], runt[:, :], gate[:, :], ALU.add))
                link(V.tensor_scalar(runt[:, :], runt[:, :], 1.0, None, ALU.max))
                to_pe(V.reciprocal(runf[:, :], runt[:, :]))

            def take_weights():
                from_pe()
                link(V.tensor_copy(wcol[:, :], psP[:, 0:TILES]))

            def steps_needed():
                from_pe()
                link(V.tensor_copy(need[:, 0, :], psP[0:1, 0:BLOCKS]))
                link(V.tensor_copy(need_i[:, 0, :], need[:, 0, :]))
                link(V.tensor_scalar(need_i[:, 1, :], need_i[:, 0, :], 9, None, ALU.arith_shift_right))
                link(V.tensor_scalar(need[:, 0, :], need[:, 0, :], float(LASTROW), None, ALU.is_ge))
                link(V.tensor_copy(need[:, 1, :], need_i[:, 1, :]))
                link(V.tensor_tensor(need[:, 1, :], need[:, 1, :], need[:, 0, :], ALU.add))
                link(V.tensor_scalar(need[:, 1, :], need[:, 1, :], 1.0, float(STEPS), ALU.add, ALU.min))
                V.tensor_copy(need_i[:, 1, :], need[:, 1, :]).then_inc(s_need, 1)

            links = (take_keys, run_lengths, join_runs, run_weights)

            def select(st):
                u = st.slot
                dve.wait_ge(spread, st.nth(1, 1))
                d = cold[:, bass.ds(st.nth(EDGE), EDGE)].rearrange("p (k a) -> p k a", a=1).broadcast_to([P, EDGE, P])
                V.tensor_tensor(smat[u % 2][:, :, :], psR[:, 0:EDGE * P].rearrange("p (k e) -> p k e", k=EDGE), d,
                                ALU.is_equal).then_inc(s_ready, 1)

            def split(st, j):
                pos, pair, edge, v = j
                if st.is_split(pos):
                    n = KC if pair is None else 2 * KC
                    dve.wait_ge(hT_ready, st.job(pos, 1))
                    wait(dve, prods, st.job(pos, 1 - SLOTS))
                    V.tensor_tensor(hT_b[v % 2][:, 0:n, :], psT[v % 2][:, 0:n, :], hT_a[v][:, 0:n, :].bitcast(F32),
                                    ALU.subtract).then_inc(hb_ready, 1)

            def split_after(st, j):
                nxt, p = (st, j[0] + 1) if j[0] + 1 < len(st.jobs()) else (st.after(1), 0)
                if not (st.turn is None and st.base == STEPS - 1 and p == 0):
                    split(nxt, nxt.jobs()[p])

            def finish(st, j):
                pos, pair, edge, v = j
                u = st.slot
                dve.wait_ge(prods, st.job(pos, 1))
                if pair is not None:
                    if pair == 0:
                        if not (st.turn is None and st.base < 2):
                            old = st.after(-2)
                            dve.wait_ge(x_out[old.slot], old.use(16, 16))
                    V.scalar_tensor_tensor(out=xout[u % 2][:, 2 * pair:2 * pair + 2, :], in0=psO[v][:, :, :],
                                           scalar=0.0, in1=xin[u][:, 2 * pair:2 * pair + 2, :],
                                           op0=ALU.max, op1=ALU.add).then_inc(fin, 1)
                elif st.kind == MSG:
                    if edge == 0:
                        wait(dve, m_out[u], st.use(16, 0, (MSG,)))
                    V.tensor_scalar(mbuf[u][:, edge, :], psO[v][:, 0, :],
                                    wcol[:, bass.ds(st.nth(EDGE, edge), 1)], None, ALU.mult).then_inc(fin, 1)
                else:
                    if not (st.turn is None and st.base == ROOT0 - 1 and edge == EDGE - 1):
                        dve.wait_ge(carry, st.nth(EDGE, edge + 2))
                    V.scalar_tensor_tensor(out=orow[:, bass.ds(st.nth(EDGE, edge), 1), :]
                                           .rearrange("p a f -> p (a f)"), in0=psO[v][:, 0, :],
                                           scalar=0.0, in1=xg[u][:, edge, :],
                                           op0=ALU.max, op1=ALU.add).then_inc(fin, 1)

            def body(st):
                jobs, left = st.jobs(), STEPS if st.turn is not None else STEPS - st.base
                nxt, far = st.after(1), st.after(2)
                if st.turn is None and st.base == AGG0:
                    dve.wait_ge(m_in[st.slot], 16 * EDGE)
                    V.memset(mbuf[st.slot][0:1, 0, :], 0.0).then_inc(carry, 1)
                more = range(DENSE, far.tiles()) if left > 2 else ()
                if st.kind not in EDGES:
                    if st.scaled_early():
                        scales(nxt)
                    sort = (range((st.base + 1) * SORT_BLOCKS, min((st.base + 2) * SORT_BLOCKS, BLOCKS))
                            if st.kind == SORT else ())
                    for b in sort[:SORT_BLOCKS // 2]:
                        one_hot_tiles(b)
                    if left > 2:
                        ins = bn(far, range(0, DENSE))
                        if more:
                            ins = bn(far, more)
                        ins.then_inc(bn_raw, 1)
                        dve.wait_ge(bn_raw, far.lin(1, 1))
                    split_after(st, jobs[0])
                    if left > 2:
                        aggregate(far)
                    finish(st, jobs[0])
                    if st.kind == LINK:
                        links[st.nth()]()
                    for b in sort[SORT_BLOCKS // 2:]:
                        one_hot_tiles(b)
                    if left > 2:
                        scales(far)
                    split_after(st, jobs[1])
                    finish(st, jobs[1])
                    if nxt.kind == AGG:
                        select(nxt)
                    return
                split_after(st, jobs[0])
                finish(st, jobs[0])
                if st.turn is None and st.base == MSG0:
                    take_weights()
                half = DENSE // 2 if st.kind == MSG else DENSE
                ins = bn(far, range(half))
                split_after(st, jobs[1])
                finish(st, jobs[1])
                if st.scaled_early():
                    scales(nxt)
                if half < DENSE:
                    ins = bn(far, range(half, DENSE))
                split_after(st, jobs[2])
                if nxt.kind == AGG:
                    select(nxt)
                if more:
                    ins = bn(far, more)
                ins.then_inc(bn_raw, 1)
                dve.wait_ge(bn_raw, far.lin(1, 1))
                finish(st, jobs[2])
                aggregate(far)
                split_after(st, jobs[3])
                finish(st, jobs[3])
                if st.kind != MSG:
                    scales(far)
                split_after(st, jobs[4])
                finish(st, jobs[4])
                if st.turn is None and st.base == MSG0 + 1:
                    steps_needed()

            for b in range(SORT_BLOCKS):
                one_hot_tiles(b)
            dve.wait_ge(wa_ready, 1)
            V.tensor_tensor(wr_b[:, :, :], wr_sb[:, :, :], wr_a[:, :, :].bitcast(F32), ALU.subtract).then_inc(wb_ready, 1)
            run_steps(dve, pl, body)

        @block.tensor
        def _(pe):
            MM = nc.tensor.matmul
            ready = [0]

            def from_dve():
                ready[0] += 1
                pe.wait_ge(s_pv, ready[0])

            pe.wait_ge(s_pool, 9)
            from_dve()
            rowtot = total[0:BLOCKS, 0, :]
            MM(psP[0:BLOCKS, 0:R], upper[0:BLOCKS, 0:BLOCKS], rowtot, start=True, stop=True)
            MM(psP[:, 16:16 + R], ones[0:BLOCKS, :], rowtot, start=True, stop=True).then_inc(s_pp, 1)
            from_dve()
            for i, row in enumerate((rowd, rowe, rows, rowk, rowpf[:, 0, :], rowpf[:, 1, :], rowg, rowp, rowo)):
                if i >= 2:
                    from_dve()
                nc.tensor.transpose(turned_rows[i % 2][:, 0:BLOCKS], row[:, 0:P], ident[0:BLOCKS, 0:BLOCKS]).then_inc(s_pp, 1)
            from_dve()
            from_dve()

            def permute(b):
                pe.wait_ge(s_lane, b + 1)
                pe.wait_ge(s_tile, b + 1)
                MM(psR[:, 0:2 * TEVEN], lanes[:, b % SORT_RING, :],
                   tiles2[:, b % SORT_RING, :, :].rearrange("p a q -> p (a q)"),
                   start=(b == 0), stop=(b == BLOCKS - 1)).then_inc(s_perm, 1)

            def turn_keys():
                from_dve()
                nc.tensor.transpose(psP[0:TILES, 0:P], keyc[:, :], ident[:, :]).then_inc(s_pp, 1)

            def turn_ends():
                from_dve()
                for c, col in enumerate((keyr[:, 0:1], keyr[:, P - 1:P], runf[:, P - 1:P], runt[:, 0:1])):
                    ins = nc.tensor.transpose(psR[0:1, c * TILES:(c + 1) * TILES], col, ident[0:TILES, 0:TILES])
                ins.then_inc(s_pp, 1)

            def turn_carries():
                from_dve()
                for c in range(2):
                    ins = MM(psP[0:TILES, c:c + 1], link_row[:, 4 + c, 0:TILES], ones[0:1, 0:1], start=True, stop=True)
                ins.then_inc(s_pp, 1)

            def turn_weights():
                from_dve()
                nc.tensor.transpose(psP[:, 0:TILES], runf[:, :], ident[0:TILES, 0:TILES]).then_inc(s_pp, 1)

            def turn_last_dst():
                nc.tensor.transpose(psP[0:1, 0:BLOCKS], rowd[:, P - 1:P],
                                    ident[0:BLOCKS, 0:BLOCKS]).then_inc(s_pp, 1)

            links = (turn_keys, turn_ends, turn_carries, turn_weights)
            pe.wait_ge(s_wr, 16 * KC)
            pe.wait_ge(rows_made, 1)

            def turn(st, j):
                pos, pair, edge, v = j
                pe.wait_ge(normed, st.job(pos, 1))
                wait(pe, hT_ready, st.job(pos, 1 - 2))
                before = st.back(pos, 2)
                if before:
                    step, p = before
                    if step.is_split(p):
                        pe.wait_ge(hb_ready, step.nth_split(p, 1))
                for t in range(1 if pair is None else 2):
                    for k in range(KC):
                        ins = nc.tensor.transpose(psT[v % 2][:, t * KC + k, :], h[v][:, t, k * P:(k + 1) * P], ident[:, :])
                ins.then_inc(turned, 1)

            def spread_dst(st):
                if not (st.turn is None and st.base == AGG0):
                    pe.wait_ge(s_ready, st.nth())
                pe.wait_ge(e_slot, st.nth(1, 1))
                for k in range(EDGE):
                    e = eslot[st.slot][:, k:k + 1]
                    ins = nc.tensor.transpose(psR[:, k * P:(k + 1) * P], e.broadcast_to([P, P]), ident[:, :])
                ins.then_inc(spread, 1)

            def load_type(st, edge):
                return nc.tensor.value_load(tile_type_i[0:1, bass.ds(st.nth(EDGE, edge), 1)], min_val=0, max_val=R - 1)

            def product(st, j, types):
                pos, pair, edge, v = j
                if pair is None and st.kind == MSG and edge not in types:
                    types[edge] = load_type(st, edge)
                r = types.get(edge)
                pe.wait_ge(hT_ready, st.job(pos, 1))
                wait(pe, fin, st.job(pos, 1 - SLOTS))
                if pair is not None:
                    MM(psO[v][:, :, :].rearrange("p a f -> p (a f)"), ones3[:, :],
                       bias_rows[:, :, :].rearrange("p a f -> p (a f)"), start=True, stop=False, skip_group_check=True)
                    if st.is_split(pos):
                        if st.turn is None and pos == 0 and st.base == pl.first[MSG]:
                            pe.wait_ge(wb_ready, 1)
                        terms = ((hT_a, wr_a), (hT_a, wr_b), (hT_b, wr_a))
                    else:
                        terms = ((hT, wr_sb),)
                    for i, (left, right) in enumerate(terms):
                        if i == 2:
                            if st.kind == MSG and pair == 0:
                                if st.turn is None and st.base == MSG0:
                                    pe.wait_ge(s_types, 1)
                                    pe.wait_ge(s_w, 16 * KC)
                                types.update((e, load_type(st, e)) for e in range(EDGE - 1))
                            pe.wait_ge(hb_ready, st.nth_split(pos, 1))
                        for t in range(2):
                            for k in range(KC):
                                ins = MM(psO[v][:, t, :], left[v % len(left)][:, t * KC + k, :], right[:, k, :], start=False,
                                         stop=(i == len(terms) - 1 and t == 1 and k == KC - 1), skip_group_check=True)
                elif st.kind == MSG:
                    for k in range(KC):
                        ins = MM(psO[v][:, 0, :], hT[v][:, k, :], w_sb[:, bass.ds(r * F + k * R * F, F)],
                                 start=(k == 0), stop=(k == KC - 1))
                else:
                    u = st.slot
                    MM(psO[v][:, 0, :], ones3_agg[:, :], bias_rows[:, 0, :], start=True, stop=False)
                    terms = ((hT_a, wr_a), (hT_a, wr_b), (hT_b, wr_a)) if st.is_split(pos) else ((hT, wr_sb),)
                    for i, (left, right) in enumerate(terms):
                        if i == 2:
                            pe.wait_ge(hb_ready, st.nth_split(pos, 1))
                        for k in range(KC):
                            MM(psO[v][:, 0, :], left[v % len(left)][:, k, :], right[:, k, :], start=False, stop=False)
                    if edge == 0:
                        pe.wait_ge(s_ready, st.nth(1, 1))
                        pe.wait_ge(m_in[u], st.use(16 * EDGE, 16 * EDGE, (AGG,)))
                    pe.wait_ge(carry, st.nth(EDGE, edge + 1))
                    ins = MM(psO[v][:, 0, :], smat[u % 2][:, edge, :], mbuf[u][:, edge, :], start=False, stop=True)
                ins.then_inc(prods, 1)

            def body(st):
                jobs, types = st.jobs(), {}
                prev, last_type = st.after(-1) if st.base else None, {}
                if prev and prev.kind == MSG:
                    last_type[EDGE - 1] = load_type(prev, EDGE - 1)
                turn(st, jobs[0])
                if prev:
                    product(prev, prev.jobs()[-1], last_type)
                if st.kind == SORT:
                    sort = range(st.base * SORT_BLOCKS, (st.base + 1) * SORT_BLOCKS)
                    for b in sort[:SORT_BLOCKS // 2]:
                        permute(b)
                for a, b in zip(jobs[1:], jobs[:-1]):
                    turn(st, a)
                    product(st, b, types)
                    if st.turn is None and b[0] == 0 and pl.first[LINK] < st.base <= MSG0:
                        links[st.base - pl.first[LINK] - 1]()
                    if st.turn is None and b[0] == 0 and st.base == MSG0 + 1:
                        turn_last_dst()
                    if a[0] == min(2, len(jobs) - 1) and st.next_kind == AGG:
                        spread_dst(st.after(1))
                if st.kind == SORT:
                    for b in sort[SORT_BLOCKS // 2:]:
                        permute(b)

            run_steps(pe, pl, body)
            last = Step(pl, STEPS - 1)
            product(last, last.jobs()[-1], {})


_INS = ["x", "src", "dst", "edge_type_8", "L0_gnn_W", "L0_gnn_W_root", "L0_gnn_bias"]


def kernel(**inputs):
    import numpy as _np
    import concourse.bacc as _bacc
    from concourse import mybir as _mybir
    from concourse.bass_utils import run_bass_kernel_spmd as _run

    nc = _bacc.Bacc("TRN2", target_bir_lowering=False, num_devices=1)
    arrays, args = {}, []
    for name in _INS:
        a = _np.ascontiguousarray(inputs[name])
        arrays[f"in_{name}_dram"] = a
        args.append(nc.dram_tensor(f"in_{name}_dram", a.shape, _mybir.dt.from_np(a.dtype), kind="ExternalInput").ap())
    out = nc.dram_tensor("out_dram", inputs["x"].shape, _mybir.dt.float32, kind="ExternalOutput").ap()
    build(nc, *args, out)
    r = _run(nc, [arrays], core_ids=[0])
    return r.results[0]["out_dram"]
```
